# Optimizing a Trainium2 kernel written in Bass

```python
import numpy as np
import jax
import jax.numpy as jnp

def _softmax(x, axis=-1):
    return jax.nn.softmax(x, axis=axis)

def _gelu(x):
    return jax.nn.gelu(x, approximate=True)

def _silu(x):
    return jax.nn.silu(x)

def _sigmoid(x):
    return jax.nn.sigmoid(x)

def _layernorm(x, axis=-1, eps=1e-05):
    m = jnp.mean(x, axis=axis, keepdims=True)
    v = jnp.var(x, axis=axis, keepdims=True)
    return (x - m) / jnp.sqrt(v + eps)

def _scatter_add(tgt, idx, src, axis=0):
    return tgt.at[idx].add(src)

def _segment_sum(src, seg, n):
    return jax.ops.segment_sum(src, seg, n)
kernel_name = 'mk_flamingo_gated_d1_seqx_r4_30bc59'

def setup_inputs(seed: int=0):
    np.random.seed(seed)
    _w = jnp.asarray

    def _rec_inputs():
        import jax
        import jax.numpy as jnp
        _rk = jax.random.key(seed)
        x = -0.000125 + 0.9999 * jax.random.normal(jax.random.fold_in(_rk, 1), (32, 112, 512), jnp.float32)
        _lenS = 112 - jax.random.randint(jax.random.fold_in(_rk, 7), (32,), 0, max(1, 112 // 4) + 1, jnp.int32)
        _lenS2 = 375 - jax.random.randint(jax.random.fold_in(_rk, 8), (32,), 0, max(1, 375 // 4) + 1, jnp.int32)
        _ctx_2048P = jax.random.normal(jax.random.fold_in(_rk, 11), (32, 16, 512), jnp.float32)
        _ctx_2048c = jax.random.dirichlet(jax.random.fold_in(_rk, 511), 0.3 * jnp.ones((16,), jnp.float32), (32, 375))
        _ctx_2048t = jnp.einsum('bsk,bkd->bsd', _ctx_2048c, _ctx_2048P)
        _ctx_2048t = _ctx_2048t * jax.lax.rsqrt(jnp.mean(jnp.square(_ctx_2048t)) + 1e-12) * 0.953939
        ctx_2048 = -0.000514642 + 1.00011 * (_ctx_2048t + 0.3 * jax.random.normal(jax.random.fold_in(_rk, 611), (32, 375, 512), jnp.float32))
        _validS = jnp.arange(112)[None, :] < _lenS[:, None]
        _validS2 = jnp.arange(375)[None, :] < _lenS2[:, None]
        _causal = jnp.tril(jnp.ones((112, 112), dtype=bool))
        mask_BxS2_bk0 = jnp.logical_not(jnp.broadcast_to(_validS2[:, :], (32, 375)))
        _g = jax.random.normal(jax.random.fold_in(_rk, 9001), (2, 1), jnp.float32)
        _g = jnp.sign(_g) * jnp.maximum(jnp.abs(_g), 1.0) + (_g == 0) * 1.0
        g_xattn = _g[0]
        g_ffn = _g[1]
        return (x, ctx_2048, mask_BxS2_bk0, g_xattn, g_ffn)
    x, ctx_2048, mask_BxS2_bk0, g_xattn, g_ffn = _rec_inputs()

    def _L0_xattn_setup():
        import jax, jax.numpy as jnp
        import numpy as np
        key = jax.random.key(seed)
        k1, k2, k3 = jax.random.split(key, 3)
        B, S, D, M = (8, 512, 512, 128)
        hidden_states = jax.random.normal(k1, (B, S, D), dtype=jnp.float32)
        memory_tokens = jax.random.normal(k2, (B, M, D), dtype=jnp.float32)
        memory_mask = jax.random.randint(k3, (B, M), 0, 2).astype(jnp.bool_)
        return {'hidden_states': hidden_states, 'memory_tokens': memory_tokens, 'memory_mask': memory_mask}
    _L0_xattn_all = _L0_xattn_setup()
    _L0_xattn_in = {k: v for k, v in _L0_xattn_all.items() if k in ()}
    del _L0_xattn_all

    def _L0_ffn_setup():
        import jax, jax.numpy as jnp
        import numpy as np
        B, S, H, E = (4, 512, 512, 8)
        key = jax.random.key(seed)
        k1, k2, k3 = jax.random.split(key, 3)
        x = jax.random.normal(k1, (B, S, H), dtype=jnp.float32)
        Wg = jax.random.normal(k2, (H, E), dtype=jnp.float32) * 0.02
        W = jax.random.normal(k3, (E, H, H), dtype=jnp.float32) * 0.02
        b = jnp.zeros((E, H), dtype=jnp.float32)
        return {'x': x, 'Wg': Wg, 'W': W, 'b': b}
    _L0_ffn_all = _L0_ffn_setup()
    _L0_ffn_in = {k: v for k, v in _L0_ffn_all.items() if k in ('Wg', 'W', 'b')}
    del _L0_ffn_all
    return {'x': x, 'ctx_2048': ctx_2048, 'mask_BxS2_bk0': mask_BxS2_bk0, 'g_xattn': g_xattn, 'g_ffn': g_ffn, 'L0_ffn_Wg': _L0_ffn_in['Wg'], 'L0_ffn_W': _L0_ffn_in['W'], 'L0_ffn_b': _L0_ffn_in['b']}

def reference(x, ctx_2048, mask_BxS2_bk0, g_xattn, g_ffn, L0_ffn_Wg, L0_ffn_W, L0_ffn_b):
    import jax
    import jax.numpy as jnp

    def _L0_xattn_ref(hidden_states, memory_tokens, memory_mask):
        import jax, jax.numpy as jnp
        import numpy as np
        B, S, D = hidden_states.shape
        scale = 1.0 / jnp.sqrt(jnp.asarray(D, hidden_states.dtype))
        scores = jnp.einsum('bsd,bmd->bsm', hidden_states, memory_tokens) * scale
        neg_inf = jnp.asarray(-1e+30, scores.dtype)
        scores = jnp.where(memory_mask[:, None, :], scores, neg_inf)
        attn = jax.nn.softmax(scores, axis=-1)
        readout = jnp.einsum('bsm,bmd->bsd', attn, memory_tokens)
        valid_b = jnp.any(memory_mask, axis=-1)
        out = jnp.where(valid_b[:, None, None], readout, jnp.zeros_like(readout))
        return out

    def _L0_ffn_ref(x, Wg, W, b):
        import jax, jax.numpy as jnp
        import numpy as np
        B, S, H, E = (4, 512, 512, 8)
        logits = jnp.einsum('bsh,he->bse', x, Wg)
        probs = jax.nn.softmax(logits, axis=-1)
        idx = jnp.argmax(probs, axis=-1)
        onehot = jax.nn.one_hot(idx, E, dtype=x.dtype)
        combine = onehot * probs
        y = jnp.einsum('bsh,ehd->bsed', x, W) + b
        out = jnp.einsum('bsed,bse->bsd', y, combine)
        return out
    x = x + jnp.tanh(g_xattn[0]) * _L0_xattn_ref(_layernorm(x, axis=-1), ctx_2048, mask_BxS2_bk0)
    x = x + jnp.tanh(g_ffn[0]) * _L0_ffn_ref(_layernorm(x, axis=-1), L0_ffn_Wg, L0_ffn_W, L0_ffn_b)
    return x

_drawn_inputs = setup_inputs


def setup_inputs(seed=0):
    import zlib

    import numpy as np

    out = dict(_drawn_inputs(seed))
    spreads = {'L0_ffn_b': (0.0, 0.409)}
    factors = {}
    for name, (base, spread) in spreads.items():
        noise = np.random.default_rng([zlib.crc32(name.encode()), seed]).standard_normal(out[name].shape)
        drawn = base * np.exp(spread * noise) if base else spread * noise
        out[name] = jnp.asarray(drawn.astype(out[name].dtype))
    for name, factor in factors.items():
        out[name] = (out[name] * factor).astype(out[name].dtype)
    return out
```

```python
from contextlib import ExitStack

import concourse.bass as bass
from concourse import mybir

F32 = mybir.dt.float32
BF16 = mybir.dt.bfloat16
I32 = mybir.dt.int32
U32 = mybir.dt.uint32
U8 = mybir.dt.uint8
ALU = mybir.AluOpType
ACT = mybir.ActivationFunctionType
AX = mybir.AxisListType

P = 128
EPS = 1e-5
MASKED = -float(2**104)
TURN = 4


class Stage:

    def __init__(self, eng, name, shift):
        self.eng, self.reg = eng, eng.alloc_register(name)
        eng.reg_mov(self.reg, TURN + shift + 1)

    def number(self, j):
        return j.at + 1 if j.turn is None else self.eng.snap(self.reg)

    def begin(self, j):
        if j.turn is not None:
            self.eng.reg_add(self.reg, self.reg, 1)


class Count:

    def __init__(self, at, turn=None):
        self.at, self.turn = at, turn

    def plus(self, n):
        return Count(self.at + n, self.turn)

    def times(self, factor, more=0):
        if self.turn is None:
            return factor * self.at + more
        return self.turn * (factor * TURN) + (factor * self.at + more)

    def rounds(self, slots):
        if self.turn is None:
            return self.at // slots
        return self.turn * (TURN // slots) + self.at // slots

    def slot(self, slots):
        return self.at % slots

    def at_least(self, n):
        least = self.at if self.turn is None else TURN + self.at
        assert self.turn is None or least >= n
        return least >= n

    def within(self, n):
        return self.turn is not None or 0 <= self.at < n


def run(eng, first, last, body):
    loop_from, loop_to = TURN, last // TURN * TURN - (TURN if last % TURN == 0 else 0)
    loop_to = min(loop_to, (last - 4) // TURN * TURN)
    for n in range(first, loop_from):
        body(Count(n))
    with eng.Fori(1, loop_to // TURN) as turn:
        for at in range(TURN):
            body(Count(at, turn))
    for n in range(loop_to, last):
        body(Count(n))


def build(nc, x, ctx, mask, g_attn, g_ffn, w_gate, w_exp, b_exp, out):
    B, S, D = x.shape
    M = ctx.shape[1]
    E = w_gate.shape[1]
    N = B * S
    KC = D // P
    MC = 3
    MP = M // MC
    SCALE = 1.0 / float(D) ** 0.5
    REGION = 4096
    TILES = (N + E * (P - 1)) // P
    NO_TOKEN = N
    LIST = E * REGION + P
    assert M == MC * MP and MP <= P and REGION >= N + P and B % TURN == 0 and S < P

    x_rows = x.rearrange("b s d -> (b s) d")
    mid = nc.dram_tensor("mid_rows", (N + 1, D), F32, kind="Internal").ap()
    lst = nc.dram_tensor("token_list", (LIST, 4), I32, kind="Internal").ap()

    with ExitStack() as stack:
        def sb(name, shape, dt=F32):
            return stack.enter_context(nc.sbuf_tensor(name, shape, dt))

        def ps(name):
            return stack.enter_context(nc.psum_tensor(name, [P, 512], F32))

        def sem(name):
            return stack.enter_context(nc.semaphore(name))

        ident = sb("ident", [P, P])
        ones = sb("ones", [P, P])
        ones_bf = sb("ones_bf", [P, P], BF16)
        before = sb("before", [P, P], BF16)
        half = sb("half", [P, 1])
        eps = sb("eps", [P, 1])
        minus = sb("minus", [P, 1])
        token_ids = sb("token_ids", [P, B], I32)
        rev = sb("rev", [P, E])
        upto = sb("upto", [1, E, E])
        tile_no = sb("tile_no", [1, TILES, E])
        tile_row = sb("tile_row", [1, TILES])
        fill = sb("fill", [P, LIST // P * 4], I32)
        fill_rows = fill[:, :].rearrange("p (r c) -> p r c", c=4)
        zero_row = sb("zero_row", [1, D])
        w_sb = sb("w_sb", [P, E * KC * D])
        wg_sb = sb("wg_sb", [P, KC, E])
        b_raw = sb("b_raw", [E * KC, P])
        b_part = [sb(f"b_part{i}", [E * KC, P], BF16) for i in range(3)]
        b_rest = [sb(f"b_rest{i}", [E * KC, P]) for i in range(2)]
        b3 = sb("b3", [3, E * D], BF16)
        mask_u8 = sb("mask_u8", [B, M], U8)
        mask_add = sb("mask_add", [B, M], BF16)
        mask_row = sb("mask_row", [1, B * M], BF16)
        any_valid = sb("any_valid", [B, 1])
        any_diag = sb("any_diag", [B, B])
        gate_in = sb("gate_in", [P, 2])
        gate_th = sb("gate_th", [P, 2])
        gv = sb("gv", [P, B])
        x_sb = sb("x_sb", [S, 4, D])
        ctx_sb = sb("ctx_sb", [MP, 4, MC, D])
        xn = sb("xn", [S, 2, D])
        xnT = sb("xnT", [P, 2, KC, S])
        ctxT = sb("ctxT", [P, 2, KC, M])
        pr = sb("pr", [S, 2, M])
        prT = sb("prT", [MP, 2, MC, S])
        x2 = sb("x2", [S, 2, D])
        xn2 = sb("xn2", [S, 2, D])
        xn2T = sb("xn2T", [P, KC, S])
        lgT = sb("lgT", [E, S])
        st1 = sb("st1", [S, 2, 6])
        mv1 = sb("mv1", [S, 2, 2])
        ve1 = sb("ve1", [S, 2, 2])
        ln1 = sb("ln1", [S, 2, 2])
        st2 = sb("st2", [S, 2, 6])
        mv2 = sb("mv2", [S, 2, 2])
        ve2 = sb("ve2", [S, 2, 2])
        nmax = sb("nmax", [S, 2])
        nbias = sb("nbias", [S, 2])
        psum_row = sb("psum_row", [S, 2])
        rinv = sb("rinv", [S, 2])
        rscale = sb("rscale", [S, 2])
        lmax = sb("lmax", [S, 1])
        lsh = sb("lsh", [S, 2, E])
        lexp = sb("lexp", [S, E])
        lsum = sb("lsum", [S, 2])
        linv = sb("linv", [S, 1])
        key = sb("key", [S, E])
        kmax = sb("kmax", [S, 1])
        hot = sb("hot", [S, 2, E], BF16)
        acc = sb("acc", [P, E], BF16)
        acc_f = sb("acc_f", [P, E])
        posm = sb("posm", [S, E])
        pos_f = sb("pos_f", [S, 1])
        pos = sb("pos", [S, 4], U32)
        pay = sb("pay", [S, 4, 4])
        pay_i = pay[:, :, :].bitcast(I32)
        cnt_i = sb("cnt_i", [1, E], I32)
        til_i = sb("til_i", [1, E], I32)
        til = sb("til", [1, E])
        cum3 = sb("cum3", [1, E, E])
        cum = sb("cum", [1, E])
        past = sb("past", [1, TILES, E])
        past_cum = sb("past_cum", [1, TILES, E])
        t_start = sb("t_start", [1, TILES])
        t_exp = sb("t_exp", [1, TILES])
        t_tmp = sb("t_tmp", [1, TILES])
        t_base = sb("t_base", [1, TILES])
        tile_base = sb("tile_base", [1, TILES], I32)
        tile_expert = sb("tile_expert", [1, TILES], I32)
        li = sb("li", [P, 4, 4], I32)
        li_f = li[:, :, :].bitcast(F32)
        li_u = li[:, :, :].bitcast(U32)
        rows = sb("rows", [P, 4, D])
        rn = sb("rn", [P, 2, D])
        rnT = sb("rnT", [P, 2, D])

        ctx_ps = [ps("ctx_ps0"), ps("ctx_ps1")]
        score_ps = [ps("score_ps0"), ps("score_ps1")]
        read_ps = ps("read_ps")
        prob_ps = ps("prob_ps")
        xT_ps = ps("xT_ps")
        small_ps = ps("small_ps")
        lgT_ps = small_ps[0:E, 0:S]
        lg_ps = small_ps[0:S, P:P + E]
        rank_ps = small_ps[0:S, P + E:P + 2 * E]
        valid_ps = small_ps[:, 256:256 + B]
        count_ps = small_ps[0:1, 300:300 + E]
        row_ps = [xT_ps, prob_ps]
        y_ps = score_ps

        gate_ld, wg_ld, b_ld, mask_ld = sem("gate_ld"), sem("wg_ld"), sem("b_ld"), sem("mask_ld")
        w_ld = sem("w_ld")
        x_ld = [sem(f"x_ld{i}") for i in range(4)]
        ctx_ld = [sem(f"ctx_ld{i}") for i in range(4)]
        fill_st, zero_st, mask_mv, b_mv = sem("fill_st"), sem("zero_st"), sem("mask_mv"), sem("b_mv")
        mid_st = [sem(f"mid_st{i}") for i in range(2)]
        list_st = [sem(f"list_st{i}") for i in range(4)]
        list_ld = [sem(f"list_ld{i}") for i in range(4)]
        row_ld = [sem(f"row_ld{i}") for i in range(4)]
        out_st = [sem(f"out_st{i}") for i in range(4)]
        const = sem("const")
        fill_ok, zero_ok, mask_ok, b_ok = sem("fill_ok"), sem("zero_ok"), sem("mask_ok"), sem("b_ok")
        set_dve, any_ok, valid_mm, th_ok, gv_ok = (sem(n) for n in ("set_dve", "any_ok", "valid_mm", "th_ok", "gv_ok"))
        st1_ok, mv1_ok, ve1_ok, rs1_ok, nm1_ok, xn_ok = (
            sem(n) for n in ("st1_ok", "mv1_ok", "ve1_ok", "rs1_ok", "nm1_ok", "xn_ok"))
        xnT_mm, xnT_ok = sem("xnT_mm"), sem("xnT_ok")
        ctxT_mm = sem("ctxT_mm")
        ctxT_act, ctxT_dve = sem("ctxT_act"), sem("ctxT_dve")
        score_mm, max_ok, nbias_ok, pr_ok = sem("score_mm"), sem("max_ok"), sem("nbias_ok"), sem("pr_ok")
        prT_mm, prT_ok, read_mm = sem("prT_mm"), sem("prT_ok"), sem("read_mm")
        rinv_ok, rscale_ok, x2_ok = sem("rinv_ok"), sem("rscale_ok"), sem("x2_ok")
        st2_ok, mv2_ok, ve2_ok, rs2_ok, nm2_ok, xn2_ok, id_ok = (
            sem(n) for n in ("st2_ok", "mv2_ok", "ve2_ok", "rs2_ok", "nm2_ok", "xn2_ok", "id_ok"))
        xn2T_mm, xn2T_ok, lgT_mm, lgT_ok, lg_mm = (
            sem(n) for n in ("xn2T_mm", "xn2T_ok", "lgT_mm", "lgT_ok", "lg_mm"))
        lmax_ok, lsh_ok, lsum_ok, key_ok, kmax_ok, hot_ok = (
            sem(n) for n in ("lmax_ok", "lsh_ok", "lsum_ok", "key_ok", "kmax_ok", "hot_ok"))
        linv_ok, scale_ok, rank_mm, acc_ok, posm_ok, posf_ok, pos_ok = (
            sem(n) for n in ("linv_ok", "scale_ok", "rank_mm", "acc_ok", "posm_ok", "posf_ok", "pos_ok"))
        count_mm, map_step, map_ok = sem("count_mm"), sem("map_step"), sem("map_ok")
        rn_ok, rnT_mm, rnT_ok, y_mm, y_ok = (sem(n) for n in ("rn_ok", "rnT_mm", "rnT_ok", "y_mm", "y_ok"))

        CONSTS = 14
        block = stack.enter_context(nc.Block())

        @block.sync
        def _(sp):
            def load(j):
                sp.dma_start(x_sb[:, j.slot(4), :], x_rows[bass.ds(j.times(S), S), :]).then_inc(x_ld[j.slot(4)], 16)
                sp.dma_start(ctx_sb[:, j.slot(4), :, :],
                             ctx[bass.ds(j.times(1), 1), :, :].rearrange("o (c p) d -> p (o c) d", c=MC)
                             ).then_inc(ctx_ld[j.slot(4)], 16)

            sp.dma_start(mask_u8[:, :], mask).then_inc(mask_ld, 16)
            load(Count(0))
            sp.dma_start(gate_in[:, 0:1], g_attn.rearrange("(a b) -> a b", a=1).to_broadcast([P, 1])).then_inc(gate_ld, 16)
            sp.dma_start(gate_in[:, 1:2], g_ffn.rearrange("(a b) -> a b", a=1).to_broadcast([P, 1])).then_inc(gate_ld, 16)
            load(Count(1))
            sp.wait_ge(mask_ok, 2)
            sp.dma_start(mask_row[:, :].rearrange("o (b m) -> o b m", b=B), mask_add[:, :]).then_inc(mask_mv, 16)
            sp.dma_start(wg_sb[:, :, :], w_gate.rearrange("(k p) e -> p k e", p=P)).then_inc(wg_ld, 16)
            sp.dma_start(b_raw[:, :], b_exp.rearrange("e (c f) -> (e c) f", f=P)).then_inc(b_ld, 16)
            load(Count(2))
            load(Count(3))
            sp.wait_ge(fill_ok, 2)
            sp.dma_start(lst.rearrange("(p r) c -> p (r c)", p=P), fill[:, :]).then_inc(fill_st, 16)
            sp.wait_ge(zero_ok, 1)
            sp.dma_start(mid[N:N + 1, :], zero_row[:, :]).then_inc(zero_st, 16)
            for i in range(3):
                sp.wait_ge(b_ok, (1, 3, 5)[i])
                sp.dma_start(b3[i:i + 1, :].rearrange("o (a f) -> o a f", f=P), b_part[i][:, :]).then_inc(b_mv, 16)

            def batch(i):
                sp.dma_start(w_sb[:, bass.ds(i.times(D), D)], w_exp[bass.ds(i.times(P), P), :]).then_inc(w_ld, 16)
                sp.wait_ge(x2_ok, i.times(1, 1))
                sp.dma_start(mid[bass.ds(i.times(S), S), :], x2[:, i.slot(2), :]).then_inc(mid_st[i.slot(2)], 16)
                if i.plus(4).within(B):
                    load(i.plus(4))

            run(sp, 0, B, batch)
            for s in range(2):
                sp.wait_ge(mid_st[s], 16 * (B // 2))
            for s in range(4):
                sp.wait_ge(list_st[s], 16 * (B // 4))
            sp.wait_ge(map_ok, 2)

            def tile(t):
                base = sp.value_load(tile_base[0:1, bass.ds(t.times(1), 1)], min_val=0, max_val=LIST - P)
                if t.at_least(4):
                    sp.wait_ge(out_st[t.slot(4)], t.rounds(4) * 16)
                sp.dma_start(li[:, t.slot(4), :], lst[bass.ds(base, P), :]).then_inc(list_ld[t.slot(4)], 16)

            run(sp, 0, TILES, tile)
            for s in range(4):
                sp.wait_ge(out_st[s], 16 * ((TILES - s + 3) // 4))

        @block.gpsimd
        def _(pool):
            pool.memset(ident[:, :], 0.0).then_inc(const, 1)
            pool.memset(ones_bf[:, :], 1.0).then_inc(const, 1)
            pool.memset(ones[:, :], 1.0).then_inc(const, 1)
            pool.memset(half[:, :], -0.5).then_inc(const, 1)
            pool.memset(eps[:, :], EPS).then_inc(const, 1)
            pool.memset(minus[:, :], -1.0).then_inc(const, 1)
            pool.wait_ge(const, 6)
            pool.affine_select(out=ident[:, :], in_=ident[:, :], compare_op=ALU.not_equal, fill=1.0, base=0,
                               pattern=[[-1, P]], channel_multiplier=1).then_inc(const, 1)

            filing = Stage(pool, "filing", -2)
            gathering = Stage(pool, "gathering", 2)
            scattering = Stage(pool, "scattering", 0)

            def spread(j, mv, ve, rstd, shift, mv_ok, ve_ok, rs_ok, nm_ok):
                pool.wait_ge(mv_ok, j.times(1, 1))
                pool.tensor_tensor(ve[:, 0:1], mv[:, 1:2], eps[0:S, :], ALU.add).then_inc(ve_ok, 1)
                pool.tensor_tensor(ve[:, 1:2], mv[:, 0:1], minus[0:S, :], ALU.mult).then_inc(ve_ok, 1)
                pool.wait_ge(ve_ok, j.times(2, 2))
                pool.tensor_tensor(rstd, ve[:, 0:1], half[0:S, :], ALU.pow).then_inc(rs_ok, 1)
                pool.wait_ge(rs_ok, j.times(1, 1))
                pool.tensor_tensor(shift, ve[:, 1:2], rstd, ALU.mult).then_inc(nm_ok, 1)

            def stats1(j):
                a = j.slot(2)
                if j.at_least(2):
                    pool.wait_ge(xn_ok, j.times(1, -1))
                spread(j, mv1[:, a, :], ve1[:, a, :], ln1[:, a, 0:1], ln1[:, a, 1:2], mv1_ok, ve1_ok, rs1_ok, nm1_ok)

            def stats2(j):
                a, b = j.slot(2), j.slot(4)
                if j.at_least(4):
                    pool.wait_ge(list_st[b], j.rounds(4) * 16)
                pool.tensor_copy(pay_i[:, b, 0:1], token_ids[0:S, bass.ds(j.times(1), 1)]).then_inc(id_ok, 1)
                spread(j, mv2[:, a, :], ve2[:, a, :], pay[:, b, 2:3], pay[:, b, 3:4], mv2_ok, ve2_ok, rs2_ok, nm2_ok)

            def file(j):
                now = filing.number(j)
                pool.wait_ge(pos_ok, now)
                pool.wait_ge(scale_ok, now)
                filing.begin(j)
                pool.indirect_dma_start(lst, bass.IndirectOffsetOnAxis(pos[:, j.slot(4):j.slot(4) + 1], 0),
                                        pay_i[:, j.slot(4), :], None).then_inc(list_st[j.slot(4)], 16)

            pool.iota(token_ids[:, :], [[S, B]], base=0, channel_multiplier=1).then_inc(const, 1)
            pool.memset(zero_row[:, :], 0.0).then_inc(zero_ok, 1)
            pool.affine_select(out=before[:, :], in_=ones_bf[:, :], compare_op=ALU.is_gt, fill=0.0, base=0,
                               pattern=[[1, P]], channel_multiplier=-1).then_inc(const, 1)
            pool.iota(rev[:, :], [[-1, E]], base=E, channel_multiplier=0,
                      allow_small_or_imprecise_dtypes=True).then_inc(const, 1)
            pool.iota(acc_f[:, :], [[REGION, E]], base=0, channel_multiplier=0,
                      allow_small_or_imprecise_dtypes=True).then_inc(const, 1)
            pool.wait_ge(const, 11)
            pool.affine_select(out=acc[:, :], in_=acc_f[:, :], compare_op=ALU.is_ge, fill=0.0, base=-(P - 1),
                               pattern=[[0, E]], channel_multiplier=1).then_inc(acc_ok, 1)
            pool.affine_select(out=upto[:, :, :], in_=ones[0:1, 0:E * E].rearrange("o (f e) -> o f e", e=E),
                               compare_op=ALU.is_ge, fill=0.0, base=0,
                               pattern=[[1, E], [-1, E]], channel_multiplier=0).then_inc(const, 1)
            pool.iota(tile_no[:, :, :], [[1, TILES], [0, E]], base=0, channel_multiplier=0,
                      allow_small_or_imprecise_dtypes=True).then_inc(const, 1)
            pool.iota(tile_row[:, :], [[P, TILES]], base=0, channel_multiplier=0,
                      allow_small_or_imprecise_dtypes=True).then_inc(const, 1)
            pool.memset(fill[:, :], 0).then_inc(fill_ok, 1)
            pool.wait_ge(fill_ok, 1)
            pool.memset(fill_rows[:, :, 0:1], NO_TOKEN).then_inc(fill_ok, 1)

            def batch(i):
                if i.plus(3).within(B):
                    stats1(i.plus(3))
                if i.plus(-2).within(B):
                    if i.plus(-2).at == 0 and i.turn is None:
                        pool.wait_ge(fill_st, 16)
                    file(i.plus(-2))
                if i.within(B):
                    stats2(i)

            run(pool, -3, B + 2, batch)
            pool.wait_ge(zero_st, 16)
            for s in range(2):
                pool.wait_ge(mid_st[s], 16 * (B // 2))

            def gather(t):
                b = t.slot(4)
                pool.wait_ge(list_ld[b], gathering.number(t) * 4 + (12 - 4 * b) if t.turn is not None
                             else t.rounds(4) * 16 + 16)
                gathering.begin(t)
                pool.indirect_dma_start(rows[:, b, :], None, mid,
                                        bass.IndirectOffsetOnAxis(li_u[:, b, 0:1], 0)).then_inc(row_ld[b], 16)

            def scatter(t):
                b = t.slot(4)
                pool.wait_ge(y_ok, scattering.number(t))
                scattering.begin(t)
                pool.indirect_dma_start(out, bass.IndirectOffsetOnAxis(li_u[:, b, 0:1], 0), rows[:, b, :], None,
                                        bounds_check=N - 1, oob_is_err=False).then_inc(out_st[b], 16)

            def tile(i):
                if i.plus(2).within(TILES):
                    gather(i.plus(2))
                if i.within(TILES):
                    scatter(i)

            run(pool, -2, TILES, tile)

        @block.scalar
        def _(act):
            act.wait_ge(gate_ld, 32)
            act.activation(gate_th[:, :], gate_in[:, :], ACT.Tanh).then_inc(th_ok, 1)

            def ctx_part(j, k):
                act.wait_ge(ctxT_mm, j.times(4, k + 1))
                if k == 0 and j.at_least(2):
                    act.wait_ge(score_mm, j.times(1, -1))
                act.activation(ctxT[:, j.slot(2), k, :], ctx_ps[k % 2][:, 0:M], ACT.Copy).then_inc(ctxT_act, 1)

            def batch(i):
                j = i.plus(-1)
                if j.within(B):
                    act.wait_ge(xn2T_mm, j.times(1, 1))
                    if j.at_least(1):
                        act.wait_ge(lgT_mm, j.times(1))
                    act.activation(xn2T[:, :, :].rearrange("p k s -> p (k s)"), xT_ps[:, 0:KC * S], ACT.Copy
                                   ).then_inc(xn2T_ok, 1)
                j = i.plus(-2)
                if j.within(B):
                    act.wait_ge(lsh_ok, j.times(1, 1))
                    act.activation(lexp[:, :], lsh[:, j.slot(2), :], ACT.Exp,
                                   accum_out=lsum[:, j.slot(2):j.slot(2) + 1]).then_inc(lsum_ok, 1)
                j = i.plus(2)
                if j.within(B):
                    ctx_part(j, 0)
                    ctx_part(j, 2)
                j = i.plus(-1)
                if j.within(B):
                    act.wait_ge(lgT_mm, j.times(1, 1))
                    if j.at_least(1):
                        act.wait_ge(lg_mm, j.times(1))
                    act.activation(lgT[:, :], lgT_ps, ACT.Copy).then_inc(lgT_ok, 1)
                j = i.plus(2)
                if j.within(B):
                    act.wait_ge(xnT_mm, j.times(1, 1))
                    act.activation(xnT[:, j.slot(2), :, :].rearrange("p k s -> p (k s)"), xT_ps[:, 0:KC * S],
                                   ACT.Copy).then_inc(xnT_ok, 1)
                j = i.plus(1)
                if j.within(B):
                    a = j.slot(2)
                    act.wait_ge(nbias_ok, j.times(1, 1))
                    if j.at_least(2):
                        act.wait_ge(prT_mm, j.times(1, -1))
                        act.wait_ge(rinv_ok, j.times(1, -1))
                    act.activation(pr[:, a, :], score_ps[a][0:S, 0:M], ACT.Exp, bias=nbias[:, a:a + 1], scale=SCALE,
                                   accum_out=psum_row[:, a:a + 1]).then_inc(pr_ok, 1)

            run(act, -2, B + 2, batch)

            def tile(t):
                act.wait_ge(row_ld[t.slot(4)], t.rounds(4) * 16 + 16)
                act.wait_ge(list_ld[t.slot(4)], t.rounds(4) * 16 + 16)
                if t.at_least(2):
                    act.wait_ge(rnT_mm, t.times(1, -1))
                act.activation(rn[:, t.slot(2), :], rows[:, t.slot(4), :], ACT.Identity,
                               bias=li_f[:, t.slot(4), 3:4], scale=li_f[:, t.slot(4), 2:3]).then_inc(rn_ok, 1)

            run(act, 0, TILES, tile)

        @block.vector
        def _(dve):
            dve.wait_ge(mask_ld, 16)
            dve.tensor_scalar(mask_add[:, :], mask_u8[:, :], -1.0, -MASKED, ALU.add, ALU.mult).then_inc(mask_ok, 1)
            dve.tensor_reduce(any_valid[:, :], mask_u8[:, :], AX.X, ALU.max).then_inc(mask_ok, 1)

            aggregating1 = Stage(dve, "aggregating1", 3)
            aggregating2 = Stage(dve, "aggregating2", 0)

            def stats1(j):
                a = j.slot(2)
                dve.wait_ge(x_ld[j.slot(4)], j.rounds(4) * 16 + 16)
                dve.bn_stats(st1[:, a, :], x_sb[:, j.slot(4), :]).then_inc(st1_ok, 1)
                now = aggregating1.number(j)
                if j.at_least(2):
                    dve.wait_ge(nm1_ok, j.times(1, -1))
                dve.wait_ge(st1_ok, now)
                aggregating1.begin(j)
                dve.bn_aggr(mv1[:, a, :], st1[:, a, :]).then_inc(mv1_ok, 1)

            def apply1(j):
                a = j.slot(2)
                dve.wait_ge(nm1_ok, j.times(1, 1))
                if j.at_least(2):
                    dve.wait_ge(xnT_mm, j.times(1, -1))
                dve.tensor_scalar(xn[:, a, :], x_sb[:, j.slot(4), :], ln1[:, a, 0:1], ln1[:, a, 1:2],
                                  ALU.mult, ALU.add).then_inc(xn_ok, 1)

            def apply2(j):
                a, b = j.slot(2), j.slot(4)
                dve.wait_ge(nm2_ok, j.times(1, 1))
                if j.at_least(2):
                    dve.wait_ge(xn2T_mm, j.times(1, -1))
                dve.tensor_scalar(xn2[:, a, :], x2[:, a, :], pay[:, b, 2:3], pay[:, b, 3:4],
                                  ALU.mult, ALU.add).then_inc(xn2_ok, 1)

            def ctx_part(j, k):
                dve.wait_ge(ctxT_mm, j.times(4, k + 1))
                if k == 1 and j.at_least(2):
                    dve.wait_ge(score_mm, j.times(1, -1))
                dve.tensor_copy(ctxT[:, j.slot(2), k, :], ctx_ps[k % 2][:, 0:M]).then_inc(ctxT_dve, 1)

            def set_up():
                dve.wait_ge(mask_ok, 2)
                dve.wait_ge(const, 11)
                dve.tensor_scalar(any_diag[:, :], ident[0:B, 0:B], any_valid[:, :], None, ALU.mult).then_inc(any_ok, 1)
                dve.wait_ge(b_ld, 16)
                dve.tensor_copy(b_part[0][:, :], b_raw[:, :]).then_inc(b_ok, 1)
                dve.wait_ge(b_ok, 1)
                dve.tensor_tensor(b_rest[0][:, :], b_raw[:, :], b_part[0][:, :], ALU.subtract).then_inc(b_ok, 1)
                dve.wait_ge(b_ok, 2)
                dve.tensor_copy(b_part[1][:, :], b_rest[0][:, :]).then_inc(b_ok, 1)
                dve.wait_ge(b_ok, 3)
                dve.tensor_tensor(b_rest[1][:, :], b_rest[0][:, :], b_part[1][:, :], ALU.subtract).then_inc(b_ok, 1)
                dve.wait_ge(b_ok, 4)
                dve.tensor_copy(b_part[2][:, :], b_rest[1][:, :]).then_inc(b_ok, 1)
                dve.wait_ge(valid_mm, 1)
                dve.wait_ge(th_ok, 1)
                dve.tensor_scalar(gv[:, :], valid_ps, gate_th[:, 0:1], None, ALU.mult).then_inc(gv_ok, 1)
                dve.wait_ge(gv_ok, 1)
                dve.wait_ge(acc_ok, 1)

            def batch(i):
                j = i.plus(-1)
                if j.within(B):
                    apply2(j)
                j = i
                if j.within(B):
                    dve.wait_ge(prT_mm, j.times(1, 1))
                    if j.at_least(2):
                        dve.wait_ge(read_mm, j.times(1, -1))
                    dve.tensor_copy(prT[:, j.slot(2), :, :].rearrange("p c s -> p (c s)"), prob_ps[0:MP, 0:MC * S]
                                    ).then_inc(prT_ok, 1)
                j = i.plus(2)
                if j.within(B):
                    ctx_part(j, 1)
                j = i.plus(1)
                if j.within(B):
                    a = j.slot(2)
                    dve.wait_ge(score_mm, j.times(1, 1))
                    dve.tensor_reduce(nmax[:, a:a + 1], score_ps[a][0:S, 0:M], AX.X, ALU.max, negate=True
                                      ).then_inc(max_ok, 1)
                j = i.plus(2)
                if j.within(B):
                    ctx_part(j, 3)
                j = i.plus(1)
                if j.within(B):
                    a = j.slot(2)
                    dve.wait_ge(max_ok, j.times(1, 1))
                    if j.at_least(2):
                        dve.wait_ge(pr_ok, j.times(1, -1))
                    dve.tensor_scalar(nbias[:, a:a + 1], nmax[:, a:a + 1], SCALE, None, ALU.mult).then_inc(nbias_ok, 1)
                j = i.plus(-2)
                if j.within(B):
                    a, b = j.slot(2), j.slot(4)
                    dve.wait_ge(rank_mm, j.times(1, 1))
                    dve.tensor_tensor(posm[:, :], rank_ps, hot[:, a, :], ALU.mult).then_inc(posm_ok, 1)
                    dve.tensor_tensor(acc[0:S, :], acc[0:S, :], hot[:, a, :], ALU.add).then_inc(acc_ok, 1)
                    dve.wait_ge(posm_ok, j.times(1, 1))
                    dve.tensor_reduce(pos_f[:, :], posm[:, :], AX.X, ALU.add).then_inc(posf_ok, 1)
                    dve.wait_ge(lsum_ok, j.times(1, 1))
                    dve.reciprocal(linv[:, :], lsum[:, a:a + 1]).then_inc(linv_ok, 1)
                    dve.wait_ge(posf_ok, j.times(1, 1))
                    dve.wait_ge(id_ok, j.times(1, 1))
                    dve.tensor_copy(pos[:, b:b + 1], pos_f[:, :]).then_inc(pos_ok, 1)
                    dve.wait_ge(linv_ok, j.times(1, 1))
                    dve.tensor_scalar(pay[:, b, 1:2], linv[:, :], gate_th[0:S, 1:2], None, ALU.mult
                                      ).then_inc(scale_ok, 1)
                j = i.plus(2)
                if j.within(B):
                    apply1(j)
                j = i.plus(3)
                if j.within(B):
                    stats1(j)
                j = i
                if j.within(B):
                    a = j.slot(2)
                    dve.wait_ge(pr_ok, j.times(1, 1))
                    dve.reciprocal(rinv[:, a:a + 1], psum_row[:, a:a + 1]).then_inc(rinv_ok, 1)
                    dve.wait_ge(rinv_ok, j.times(1, 1))
                    dve.tensor_tensor(rscale[:, a:a + 1], rinv[:, a:a + 1], gv[0:S, bass.ds(j.times(1), 1)], ALU.mult
                                      ).then_inc(rscale_ok, 1)
                    dve.wait_ge(rscale_ok, j.times(1, 1))
                    if j.at_least(2):
                        dve.wait_ge(mid_st[a], j.rounds(2) * 16)
                    dve.wait_ge(read_mm, j.times(1, 1))
                    dve.scalar_tensor_tensor(x2[:, a, :], read_ps[0:S, :], rscale[:, a:a + 1], x_sb[:, j.slot(4), :],
                                             ALU.mult, ALU.add).then_inc(x2_ok, 1)
                    dve.wait_ge(x2_ok, j.times(1, 1))
                    dve.bn_stats(st2[:, a, :], x2[:, a, :]).then_inc(st2_ok, 1)
                    now = aggregating2.number(j)
                    if j.at_least(2):
                        dve.wait_ge(nm2_ok, j.times(1, -1))
                    dve.wait_ge(st2_ok, now)
                    aggregating2.begin(j)
                    dve.bn_aggr(mv2[:, a, :], st2[:, a, :]).then_inc(mv2_ok, 1)
                j = i.plus(-1)
                if j.within(B):
                    a = j.slot(2)
                    dve.wait_ge(lg_mm, j.times(1, 1))
                    dve.tensor_reduce(lmax[:, :], lg_ps, AX.X, ALU.max).then_inc(lmax_ok, 1)
                    dve.wait_ge(lmax_ok, j.times(1, 1))
                    if j.at_least(2):
                        dve.wait_ge(lsum_ok, j.times(1, -1))
                    dve.tensor_scalar(lsh[:, a, :], lg_ps, lmax[:, :], None, ALU.subtract).then_inc(lsh_ok, 1)
                    dve.wait_ge(lsh_ok, j.times(1, 1))
                    dve.scalar_tensor_tensor(key[:, :], lsh[:, a, :], 0.0, rev[0:S, :], ALU.is_ge, ALU.mult
                                             ).then_inc(key_ok, 1)
                    dve.wait_ge(key_ok, j.times(1, 1))
                    dve.tensor_reduce(kmax[:, :], key[:, :], AX.X, ALU.max).then_inc(kmax_ok, 1)
                    dve.wait_ge(kmax_ok, j.times(1, 1))
                    dve.tensor_scalar(hot[:, a, :], key[:, :], kmax[:, :], None, ALU.is_equal).then_inc(hot_ok, 1)
                if i.turn is None and i.at == -1:
                    set_up()

            run(dve, -3, B + 2, batch)

            steps = [0]

            def step(ins):
                steps[0] += 1
                ins.then_inc(map_step, 1)
                dve.wait_ge(map_step, steps[0])

            dve.wait_ge(count_mm, 1)
            step(dve.tensor_scalar(cnt_i[:, :], count_ps, float(P - 1), None, ALU.add))
            step(dve.tensor_scalar(til_i[:, :], cnt_i[:, :], 7, None, ALU.arith_shift_right))
            step(dve.tensor_copy(til[:, :], til_i[:, :]))
            step(dve.tensor_tensor(cum3[:, :, :], upto[:, :, :], til[:, :].rearrange("o (f e) -> o f e", f=1).to_broadcast([1, E, E]), ALU.mult))
            step(dve.tensor_reduce(cum[:, :], cum3[:, :, :], AX.X, ALU.add))
            cum_all = cum[:, :].rearrange("o (f e) -> o f e", f=1).to_broadcast([1, TILES, E])
            step(dve.tensor_tensor(past[:, :, :], tile_no[:, :, :], cum_all, ALU.is_ge))
            step(dve.tensor_tensor(past_cum[:, :, :], past[:, :, :], cum_all, ALU.mult))
            step(dve.tensor_reduce(t_exp[:, :], past[:, :, :], AX.X, ALU.add))
            step(dve.tensor_reduce(t_start[:, :], past_cum[:, :, :], AX.X, ALU.max))
            step(dve.scalar_tensor_tensor(t_tmp[:, :], t_start[:, :], -float(P), tile_row[:, :], ALU.mult, ALU.add))
            step(dve.scalar_tensor_tensor(t_base[:, :], t_exp[:, :], float(REGION), t_tmp[:, :], ALU.mult, ALU.add))
            dve.tensor_scalar(tile_base[:, :], t_base[:, :], float(E * REGION), None, ALU.min).then_inc(map_ok, 1)
            dve.tensor_scalar(tile_expert[:, :], t_exp[:, :], float(E - 1), None, ALU.min).then_inc(map_ok, 1)

            def tile(i):
                t = i.plus(1)
                if t.within(TILES):
                    dve.wait_ge(rnT_mm, t.times(1, 1))
                    if t.at_least(2):
                        dve.wait_ge(y_mm, t.times(1, -1))
                    dve.tensor_copy(rnT[:, t.slot(2), :], row_ps[t.slot(2)][:, :]).then_inc(rnT_ok, 1)
                t = i
                if t.within(TILES):
                    b = t.slot(4)
                    dve.wait_ge(y_mm, t.times(1, 1))
                    dve.scalar_tensor_tensor(rows[:, b, :], y_ps[t.slot(2)][:, :], li_f[:, b, 1:2], rows[:, b, :],
                                             ALU.mult, ALU.add).then_inc(y_ok, 1)

            run(dve, -1, TILES, tile)

        @block.tensor
        def _(pe):
            turning_logits = Stage(pe, "turning_logits", -1)

            def ctx_turn(j, k):
                if k == 0:
                    pe.wait_ge(ctx_ld[j.slot(4)], j.rounds(4) * 16 + 16)
                if k >= 2 or j.at_least(1):
                    pe.wait_ge((ctxT_act, ctxT_dve)[k % 2], j.times(2, k // 2))
                for c in range(MC):
                    last = pe.transpose(ctx_ps[k % 2][:, c * MP:(c + 1) * MP],
                                        ctx_sb[:, j.slot(4), c, k * P:(k + 1) * P], ident[0:MP, 0:MP])
                last.then_inc(ctxT_mm, 1)

            def x_turn(j):
                pe.wait_ge(xn_ok, j.times(1, 1))
                if j.turn is not None or j.at - 2 >= 1:
                    pe.wait_ge(xn2T_ok, j.times(1, -2))
                for k in range(KC):
                    last = pe.transpose(xT_ps[:, k * S:(k + 1) * S], xn[:, j.slot(2), k * P:(k + 1) * P],
                                        ident[0:S, 0:S])
                last.then_inc(xnT_mm, 1)

            def x2_turn(j):
                pe.wait_ge(xn2_ok, j.times(1, 1))
                pe.wait_ge(xnT_ok, j.times(1, 3) if j.turn is not None else min(j.at + 3, B))
                for k in range(KC):
                    last = pe.transpose(xT_ps[:, k * S:(k + 1) * S], xn2[:, j.slot(2), k * P:(k + 1) * P],
                                        ident[0:S, 0:S])
                last.then_inc(xn2T_mm, 1)

            def scores(j):
                a = j.slot(2)
                pe.wait_ge(xnT_ok, j.times(1, 1))
                pe.wait_ge(ctxT_act, j.times(2, 2))
                pe.wait_ge(ctxT_dve, j.times(2, 2))
                if j.at_least(2):
                    pe.wait_ge(pr_ok, j.times(1, -1))
                for k in range(KC):
                    pe.matmul(score_ps[a][0:S, 0:M], xnT[:, a, k, :], ctxT[:, a, k, :], start=(k == 0), stop=False)
                pe.matmul(score_ps[a][0:S, 0:M], ones_bf[0:1, 0:S], mask_row[0:1, bass.ds(j.times(M), M)],
                          start=False, stop=True).then_inc(score_mm, 1)

            def ranks(j):
                a = j.slot(2)
                pe.wait_ge(hot_ok, j.times(1, 1))
                pe.wait_ge(acc_ok, j.times(1, 1))
                pe.matmul(rank_ps, ones_bf[:, 0:S], acc[:, :], start=True, stop=False)
                pe.matmul(rank_ps, before[0:S, 0:S], hot[:, a, :], start=False, stop=True).then_inc(rank_mm, 1)

            def batch(i):
                j = i.plus(1)
                if j.within(B):
                    scores(j)
                j = i.plus(-2)
                if j.within(B):
                    ranks(j)
                j = i
                if j.within(B):
                    a = j.slot(2)
                    pe.wait_ge(pr_ok, j.times(1, 1))
                    if j.at_least(1):
                        pe.wait_ge(prT_ok, j.times(1))
                    for c in range(MC):
                        last = pe.transpose(prob_ps[0:MP, c * S:(c + 1) * S], pr[:, a, c * MP:(c + 1) * MP],
                                            ident[0:S, 0:S])
                    last.then_inc(prT_mm, 1)
                j = i.plus(-1)
                if j.within(B):
                    x2_turn(j)
                j = i.plus(2)
                if j.within(B):
                    for k in range(KC):
                        ctx_turn(j, k)
                j = i.plus(-1)
                if j.within(B):
                    pe.wait_ge(xn2T_ok, j.times(1, 1))
                    if j.at_least(1):
                        pe.wait_ge(posm_ok, j.times(1))
                    for k in range(KC):
                        last = pe.matmul(lgT_ps, wg_sb[:, k, :], xn2T[:, k, :], start=(k == 0), stop=(k == KC - 1))
                    last.then_inc(lgT_mm, 1)
                j = i.plus(2)
                if j.within(B):
                    x_turn(j)
                j = i
                if j.within(B):
                    a = j.slot(2)
                    pe.wait_ge(prT_ok, j.times(1, 1))
                    if j.at_least(1):
                        pe.wait_ge(x2_ok, j.times(1))
                    for c in range(MC):
                        last = pe.matmul(read_ps[0:S, :], prT[:, a, c, :], ctx_sb[:, j.slot(4), c, :],
                                         start=(c == 0), stop=(c == MC - 1))
                    last.then_inc(read_mm, 1)
                j = i.plus(-1)
                if j.within(B):
                    pe.wait_ge(lgT_ok, turning_logits.number(j))
                    turning_logits.begin(j)
                    pe.transpose(lg_ps, lgT[:, :], ident[0:E, 0:E]).then_inc(lg_mm, 1)

            pe.wait_ge(const, 7)
            for n in range(-2, 0):
                batch(Count(n))
                if n == -2:
                    pe.wait_ge(mask_mv, 16)
            pe.wait_ge(any_ok, 1)
            pe.matmul(valid_ps, ones[0:B, :], any_diag[:, :], start=True, stop=True).then_inc(valid_mm, 1)
            pe.wait_ge(const, CONSTS - 3)
            pe.wait_ge(wg_ld, 16)
            pe.wait_ge(gv_ok, 1)
            run(pe, 0, B + 2, batch)

            pe.wait_ge(acc_ok, B + 1)
            pe.wait_ge(posm_ok, B)
            pe.matmul(count_ps, ones_bf[0:S, 0:1], acc[0:S, :], start=True, stop=True).then_inc(count_mm, 1)
            pe.wait_ge(w_ld, 16 * B)
            pe.wait_ge(b_mv, 48)
            pe.wait_ge(map_ok, 2)

            def tile(i):
                t = i.plus(1)
                if t.within(TILES):
                    a = t.slot(2)
                    pe.wait_ge(rn_ok, t.times(1, 1))
                    if t.at_least(2):
                        pe.wait_ge(rnT_ok, t.times(1, -1))
                    for k in range(KC):
                        last = pe.transpose(row_ps[a][:, k * P:(k + 1) * P], rn[:, a, k * P:(k + 1) * P], ident[:, :])
                    last.then_inc(rnT_mm, 1)
                t = i
                if t.within(TILES):
                    a = t.slot(2)
                    expert = pe.value_load(tile_expert[0:1, bass.ds(t.times(1), 1)], min_val=0, max_val=E - 1)
                    pe.wait_ge(rnT_ok, t.times(1, 1))
                    if t.at_least(2):
                        pe.wait_ge(y_ok, t.times(1, -1))
                    for k in range(KC):
                        pe.matmul(y_ps[a][:, :], rnT[:, a, k * P:(k + 1) * P],
                                  w_sb[:, bass.ds(expert * (KC * D) + k * D, D)], start=(k == 0), stop=False)
                    pe.matmul(y_ps[a][:, :], ones_bf[0:3, :], b3[:, bass.ds(expert * D, D)],
                              start=False, stop=True).then_inc(y_mm, 1)

            run(pe, -1, TILES, tile)


_INS = ["x", "ctx_2048", "mask_BxS2_bk0", "g_xattn", "g_ffn", "L0_ffn_Wg", "L0_ffn_W", "L0_ffn_b"]


def kernel(**inputs):
    import numpy as _np
    import concourse.bacc as _bacc
    from concourse import mybir as _mybir
    from concourse.bass_utils import run_bass_kernel_spmd as _run

    nc = _bacc.Bacc("TRN2", target_bir_lowering=False, num_devices=1)
    arrays, args = {}, []
    for name in _INS:
        a = _np.ascontiguousarray(inputs[name])
        if name == "L0_ffn_W":
            a = a.reshape(-1, a.shape[-1])
        arrays[f"in_{name}"] = a
        args.append(nc.dram_tensor(f"in_{name}", a.shape, _mybir.dt.from_np(a.dtype), kind="ExternalInput").ap())
    b, s, d = inputs["x"].shape
    out = nc.dram_tensor("out_rows", (b * s, d), _mybir.dt.float32, kind="ExternalOutput").ap()
    build(nc, *args, out)
    r = _run(nc, [arrays], core_ids=[0])
    return r.results[0]["out_rows"].reshape(b, s, d)
```

```python
from contextlib import ExitStack

import concourse.bass as bass
from concourse import mybir

F32 = mybir.dt.float32
BF16 = mybir.dt.bfloat16
I32 = mybir.dt.int32
U32 = mybir.dt.uint32
U8 = mybir.dt.uint8
ALU = mybir.AluOpType
ACT = mybir.ActivationFunctionType
AX = mybir.AxisListType

P = 128
EPS = 1e-5
MASKED = -float(2**104)
TURN = 4


class Stage:

    def __init__(self, eng, name, shift):
        self.eng, self.reg = eng, eng.alloc_register(name)
        eng.reg_mov(self.reg, TURN + shift + 1)

    def number(self, j):
        return j.at + 1 if j.turn is None else self.eng.snap(self.reg)

    def begin(self, j):
        if j.turn is not None:
            self.eng.reg_add(self.reg, self.reg, 1)


class Count:

    def __init__(self, at, turn=None):
        self.at, self.turn = at, turn

    def plus(self, n):
        return Count(self.at + n, self.turn)

    def times(self, factor, more=0):
        if self.turn is None:
            return factor * self.at + more
        return self.turn * (factor * TURN) + (factor * self.at + more)

    def rounds(self, slots):
        if self.turn is None:
            return self.at // slots
        return self.turn * (TURN // slots) + self.at // slots

    def slot(self, slots):
        return self.at % slots

    def at_least(self, n):
        least = self.at if self.turn is None else TURN + self.at
        assert self.turn is None or least >= n
        return least >= n

    def within(self, n):
        return self.turn is not None or 0 <= self.at < n


def run(eng, first, last, body):
    loop_from, loop_to = TURN, last // TURN * TURN - (TURN if last % TURN == 0 else 0)
    loop_to = min(loop_to, (last - 4) // TURN * TURN)
    for n in range(first, loop_from):
        body(Count(n))
    with eng.Fori(1, loop_to // TURN) as turn:
        for at in range(TURN):
            body(Count(at, turn))
    for n in range(loop_to, last):
        body(Count(n))


def build(nc, x, ctx, mask, g_attn, g_ffn, w_gate, w_exp, b_exp, out):
    B, S, D = x.shape
    M = ctx.shape[1]
    E = w_gate.shape[1]
    N = B * S
    KC = D // P
    MC = 3
    MP = M // MC
    SCALE = 1.0 / float(D) ** 0.5
    REGION = 4096
    TILES = (N + E * (P - 1)) // P
    NO_TOKEN = N
    LIST = E * REGION + P
    assert M == MC * MP and MP <= P and REGION >= N + P and B % TURN == 0 and S < P

    x_rows = x.rearrange("b s d -> (b s) d")
    mid = nc.dram_tensor("mid_rows", (N + 1, D), F32, kind="Internal").ap()
    lst = nc.dram_tensor("token_list", (LIST, 4), F32, kind="Internal").ap()

    with ExitStack() as stack:
        def sb(name, shape, dt=F32):
            return stack.enter_context(nc.sbuf_tensor(name, shape, dt))

        def ps(name):
            return stack.enter_context(nc.psum_tensor(name, [P, 512], F32))

        def sem(name):
            return stack.enter_context(nc.semaphore(name))

        ident = sb("ident", [P, P])
        ones = sb("ones", [P, P])
        ones_bf = sb("ones_bf", [P, P], BF16)
        before = sb("before", [P, P], BF16)
        half = sb("half", [P, 1])
        eps = sb("eps", [P, 1])
        minus = sb("minus", [P, 1])
        token_ids = sb("token_ids", [P, B], I32)
        rev = sb("rev", [P, E])
        upto = sb("upto", [1, E, E])
        tile_no = sb("tile_no", [1, TILES, E])
        tile_row = sb("tile_row", [1, TILES])
        fill = sb("fill", [P, LIST // P * 4])
        fill_rows = fill[:, :].rearrange("p (r c) -> p r c", c=4)
        zero_row = sb("zero_row", [1, D])
        w_sb = sb("w_sb", [P, E * KC * D])
        wg_sb = sb("wg_sb", [P, KC, E])
        b_raw = sb("b_raw", [E * KC, P])
        b_part = [sb(f"b_part{i}", [E * KC, P], BF16) for i in range(3)]
        b_rest = [sb(f"b_rest{i}", [E * KC, P]) for i in range(2)]
        b3 = sb("b3", [3, E * D], BF16)
        mask_u8 = sb("mask_u8", [B, M], U8)
        mask_add = sb("mask_add", [B, M], BF16)
        mask_row = sb("mask_row", [1, B * M], BF16)
        any_valid = sb("any_valid", [B, 1])
        any_diag = sb("any_diag", [B, B])
        gate_in = sb("gate_in", [P, 2])
        gate_th = sb("gate_th", [P, 2])
        gv = sb("gv", [P, B])
        x_sb = sb("x_sb", [S, 4, D])
        ctx_sb = sb("ctx_sb", [MP, 4, MC, D])
        xn = sb("xn", [S, 2, D])
        xnT = sb("xnT", [P, 2, KC, S])
        ctxT = sb("ctxT", [P, 2, KC, M])
        pr = sb("pr", [S, 2, M])
        prT = sb("prT", [MP, 2, MC, S])
        x2 = sb("x2", [S, 2, D])
        xn2 = sb("xn2", [S, 2, D])
        xn2T = sb("xn2T", [P, KC, S])
        lgT = sb("lgT", [E, S])
        st1 = sb("st1", [S, 2, 6])
        mv1 = sb("mv1", [S, 2, 2])
        ve1 = sb("ve1", [S, 2, 2])
        ln1 = sb("ln1", [S, 2, 2])
        st2 = sb("st2", [S, 2, 6])
        mv2 = sb("mv2", [S, 2, 2])
        ve2 = sb("ve2", [S, 2, 2])
        nmax = sb("nmax", [S, 2])
        nbias = sb("nbias", [S, 2])
        psum_row = sb("psum_row", [S, 2])
        rinv = sb("rinv", [S, 2])
        rscale = sb("rscale", [S, 2])
        lmax = sb("lmax", [S, 1])
        lsh = sb("lsh", [S, 2, E])
        lexp = sb("lexp", [S, E])
        lsum = sb("lsum", [S, 2])
        linv = sb("linv", [S, 1])
        key = sb("key", [S, E])
        kmax = sb("kmax", [S, 1])
        hot = sb("hot", [S, 2, E], BF16)
        acc = sb("acc", [P, E], BF16)
        acc_f = sb("acc_f", [P, E])
        posm = sb("posm", [S, E])
        pos_f = sb("pos_f", [S, 1])
        pos = sb("pos", [S, 4], U32)
        pay = sb("pay", [S, 4, 4])
        cnt_i = sb("cnt_i", [1, E], I32)
        til_i = sb("til_i", [1, E], I32)
        til = sb("til", [1, E])
        cum3 = sb("cum3", [1, E, E])
        cum = sb("cum", [1, E])
        past = sb("past", [1, TILES, E])
        past_cum = sb("past_cum", [1, TILES, E])
        t_start = sb("t_start", [1, TILES])
        t_exp = sb("t_exp", [1, TILES])
        t_tmp = sb("t_tmp", [1, TILES])
        t_base = sb("t_base", [1, TILES])
        tile_base = sb("tile_base", [1, TILES], I32)
        tile_expert = sb("tile_expert", [1, TILES], I32)
        li = sb("li", [P, TILES, 4])
        take = sb("take", [P, 4], U32)
        put = sb("put", [P, 4], U32)
        rows = sb("rows", [P, 4, D])
        res = sb("res", [P, 4, D])
        rn = sb("rn", [P, 2, D])
        rnT = sb("rnT", [P, 2, D])

        ctx_ps = [ps("ctx_ps0"), ps("ctx_ps1")]
        score_ps = [ps("score_ps0"), ps("score_ps1")]
        read_ps = ps("read_ps")
        prob_ps = ps("prob_ps")
        xT_ps = ps("xT_ps")
        small_ps = ps("small_ps")
        lgT_ps = small_ps[0:E, 0:S]
        lg_ps = small_ps[0:S, P:P + E]
        rank_ps = small_ps[0:S, P + E:P + 2 * E]
        valid_ps = small_ps[:, 256:256 + B]
        count_ps = small_ps[0:1, 300:300 + E]
        row_ps = [xT_ps, prob_ps]
        y_ps = score_ps

        gate_ld, wg_ld, b_ld, mask_ld = sem("gate_ld"), sem("wg_ld"), sem("b_ld"), sem("mask_ld")
        w_ld = sem("w_ld")
        x_ld = [sem(f"x_ld{i}") for i in range(4)]
        ctx_ld = [sem(f"ctx_ld{i}") for i in range(4)]
        fill_st, zero_st, mask_mv, b_mv = sem("fill_st"), sem("zero_st"), sem("mask_mv"), sem("b_mv")
        mid_st = [sem(f"mid_st{i}") for i in range(2)]
        list_st = [sem(f"list_st{i}") for i in range(4)]
        list_ld = [sem(f"list_ld{i}") for i in range(4)]
        row_ld = [sem(f"row_ld{i}") for i in range(4)]
        out_st = [sem(f"out_st{i}") for i in range(4)]
        const = sem("const")
        fill_ok, zero_ok, mask_ok, b_ok = sem("fill_ok"), sem("zero_ok"), sem("mask_ok"), sem("b_ok")
        set_dve, any_ok, valid_mm, th_ok, gv_ok = (sem(n) for n in ("set_dve", "any_ok", "valid_mm", "th_ok", "gv_ok"))
        st1_ok, mv1_ok, ve1_ok, rs1_ok, nm1_ok, xn_ok = (
            sem(n) for n in ("st1_ok", "mv1_ok", "ve1_ok", "rs1_ok", "nm1_ok", "xn_ok"))
        xnT_mm, xnT_ok = sem("xnT_mm"), sem("xnT_ok")
        ctxT_mm = sem("ctxT_mm")
        ctxT_act, ctxT_dve = sem("ctxT_act"), sem("ctxT_dve")
        score_mm, max_ok, nbias_ok, pr_ok = sem("score_mm"), sem("max_ok"), sem("nbias_ok"), sem("pr_ok")
        prT_mm, prT_ok, read_mm = sem("prT_mm"), sem("prT_ok"), sem("read_mm")
        rinv_ok, rscale_ok, x2_ok = sem("rinv_ok"), sem("rscale_ok"), sem("x2_ok")
        st2_ok, mv2_ok, ve2_ok, rs2_ok, nm2_ok, xn2_ok, id_ok = (
            sem(n) for n in ("st2_ok", "mv2_ok", "ve2_ok", "rs2_ok", "nm2_ok", "xn2_ok", "id_ok"))
        xn2T_mm, xn2T_ok, lgT_mm, lgT_ok, lg_mm = (
            sem(n) for n in ("xn2T_mm", "xn2T_ok", "lgT_mm", "lgT_ok", "lg_mm"))
        lmax_ok, lsh_ok, lsum_ok, key_ok, kmax_ok, hot_ok = (
            sem(n) for n in ("lmax_ok", "lsh_ok", "lsum_ok", "key_ok", "kmax_ok", "hot_ok"))
        linv_ok, scale_ok, rank_mm, acc_ok, posm_ok, posf_ok, pos_ok = (
            sem(n) for n in ("linv_ok", "scale_ok", "rank_mm", "acc_ok", "posm_ok", "posf_ok", "pos_ok"))
        count_mm, map_step, map_ok = sem("count_mm"), sem("map_step"), sem("map_ok")
        take_ok, put_ok, rn_ok, rnT_mm, rnT_ok, y_mm, y_ok = (
            sem(n) for n in ("take_ok", "put_ok", "rn_ok", "rnT_mm", "rnT_ok", "y_mm", "y_ok"))

        CONSTS = 14
        block = stack.enter_context(nc.Block())

        @block.sync
        def _(sp):
            def load(j):
                sp.dma_start(x_sb[:, j.slot(4), :], x_rows[bass.ds(j.times(S), S), :]).then_inc(x_ld[j.slot(4)], 16)
                sp.dma_start(ctx_sb[:, j.slot(4), :, :],
                             ctx[bass.ds(j.times(1), 1), :, :].rearrange("o (c p) d -> p (o c) d", c=MC)
                             ).then_inc(ctx_ld[j.slot(4)], 16)

            sp.dma_start(mask_u8[:, :], mask).then_inc(mask_ld, 16)
            load(Count(0))
            sp.dma_start(gate_in[:, 0:1], g_attn.rearrange("(a b) -> a b", a=1).to_broadcast([P, 1])).then_inc(gate_ld, 16)
            sp.dma_start(gate_in[:, 1:2], g_ffn.rearrange("(a b) -> a b", a=1).to_broadcast([P, 1])).then_inc(gate_ld, 16)
            load(Count(1))
            sp.wait_ge(mask_ok, 2)
            sp.dma_start(mask_row[:, :].rearrange("o (b m) -> o b m", b=B), mask_add[:, :]).then_inc(mask_mv, 16)
            sp.dma_start(wg_sb[:, :, :], w_gate.rearrange("(k p) e -> p k e", p=P)).then_inc(wg_ld, 16)
            sp.dma_start(b_raw[:, :], b_exp.rearrange("e (c f) -> (e c) f", f=P)).then_inc(b_ld, 16)
            load(Count(2))
            load(Count(3))
            sp.wait_ge(fill_ok, 2)
            sp.dma_start(lst.rearrange("(p r) c -> p (r c)", p=P), fill[:, :]).then_inc(fill_st, 16)
            sp.wait_ge(zero_ok, 1)
            sp.dma_start(mid[N:N + 1, :], zero_row[:, :]).then_inc(zero_st, 16)
            for i in range(3):
                sp.wait_ge(b_ok, (1, 3, 5)[i])
                sp.dma_start(b3[i:i + 1, :].rearrange("o (a f) -> o a f", f=P), b_part[i][:, :]).then_inc(b_mv, 16)

            def batch(i):
                sp.dma_start(w_sb[:, bass.ds(i.times(D), D)], w_exp[bass.ds(i.times(P), P), :]).then_inc(w_ld, 16)
                sp.wait_ge(x2_ok, i.times(1, 1))
                sp.dma_start(mid[bass.ds(i.times(S), S), :], x2[:, i.slot(2), :]).then_inc(mid_st[i.slot(2)], 16)
                if i.plus(4).within(B):
                    load(i.plus(4))

            run(sp, 0, B, batch)
            for s in range(2):
                sp.wait_ge(mid_st[s], 16 * (B // 2))
            for s in range(4):
                sp.wait_ge(list_st[s], 16 * (B // 4))
            sp.wait_ge(map_ok, 2)

            def tile(t):
                base = sp.value_load(tile_base[0:1, bass.ds(t.times(1), 1)], min_val=0, max_val=LIST - P)
                if t.at_least(4):
                    sp.wait_ge(take_ok, t.times(1, -3))
                sp.dma_start(li[:, bass.ds(t.times(1), 1), :].rearrange("p o c -> p (o c)"), lst[bass.ds(base, P), :]
                             ).then_inc(list_ld[t.slot(4)], 16)

            run(sp, 0, TILES, tile)
            for s in range(4):
                sp.wait_ge(out_st[s], 16 * ((TILES - s + 3) // 4))

        @block.gpsimd
        def _(pool):
            pool.memset(ident[:, :], 0.0).then_inc(const, 1)
            pool.memset(ones_bf[:, :], 1.0).then_inc(const, 1)
            pool.memset(ones[:, :], 1.0).then_inc(const, 1)
            pool.memset(half[:, :], -0.5).then_inc(const, 1)
            pool.memset(eps[:, :], EPS).then_inc(const, 1)
            pool.memset(minus[:, :], -1.0).then_inc(const, 1)
            pool.wait_ge(const, 6)
            pool.affine_select(out=ident[:, :], in_=ident[:, :], compare_op=ALU.not_equal, fill=1.0, base=0,
                               pattern=[[-1, P]], channel_multiplier=1).then_inc(const, 1)

            filing = Stage(pool, "filing", -2)
            gathering = Stage(pool, "gathering", 3)
            scattering = Stage(pool, "scattering", 0)

            def spread(j, mv, ve, rstd, shift, mv_ok, ve_ok, rs_ok, nm_ok):
                pool.wait_ge(mv_ok, j.times(1, 1))
                pool.tensor_tensor(ve[:, 0:1], mv[:, 1:2], eps[0:S, :], ALU.add).then_inc(ve_ok, 1)
                pool.tensor_tensor(ve[:, 1:2], mv[:, 0:1], minus[0:S, :], ALU.mult).then_inc(ve_ok, 1)
                pool.wait_ge(ve_ok, j.times(2, 2))
                pool.tensor_tensor(rstd, ve[:, 0:1], half[0:S, :], ALU.pow).then_inc(rs_ok, 1)
                pool.wait_ge(rs_ok, j.times(1, 1))
                pool.tensor_tensor(shift, ve[:, 1:2], rstd, ALU.mult).then_inc(nm_ok, 1)

            def stats1(j):
                a = j.slot(2)
                if j.at_least(2):
                    pool.wait_ge(xn_ok, j.times(1, -1))
                spread(j, mv1[:, a, :], ve1[:, a, :], ln1[:, a, 0:1], ln1[:, a, 1:2], mv1_ok, ve1_ok, rs1_ok, nm1_ok)

            def name(j):
                b = j.slot(4)
                if j.at_least(4):
                    pool.wait_ge(list_st[b], j.rounds(4) * 16)
                pool.tensor_copy(pay[:, b, 0:1], token_ids[0:S, bass.ds(j.times(1), 1)]).then_inc(id_ok, 1)

            def stats2(j):
                a, b = j.slot(2), j.slot(4)
                spread(j, mv2[:, a, :], ve2[:, a, :], pay[:, b, 2:3], pay[:, b, 3:4], mv2_ok, ve2_ok, rs2_ok, nm2_ok)

            def file(j):
                now = filing.number(j)
                pool.wait_ge(pos_ok, now)
                pool.wait_ge(scale_ok, now)
                filing.begin(j)
                pool.indirect_dma_start(lst, bass.IndirectOffsetOnAxis(pos[:, j.slot(4):j.slot(4) + 1], 0),
                                        pay[:, j.slot(4), :], None).then_inc(list_st[j.slot(4)], 16)

            pool.iota(token_ids[:, :], [[S, B]], base=0, channel_multiplier=1).then_inc(const, 1)
            pool.memset(zero_row[:, :], 0.0).then_inc(zero_ok, 1)
            pool.affine_select(out=before[:, :], in_=ones_bf[:, :], compare_op=ALU.is_gt, fill=0.0, base=0,
                               pattern=[[1, P]], channel_multiplier=-1).then_inc(const, 1)
            pool.iota(rev[:, :], [[-1, E]], base=E, channel_multiplier=0,
                      allow_small_or_imprecise_dtypes=True).then_inc(const, 1)
            pool.iota(acc_f[:, :], [[REGION, E]], base=0, channel_multiplier=0,
                      allow_small_or_imprecise_dtypes=True).then_inc(const, 1)
            pool.wait_ge(const, 11)
            pool.affine_select(out=acc[:, :], in_=acc_f[:, :], compare_op=ALU.is_ge, fill=0.0, base=-(P - 1),
                               pattern=[[0, E]], channel_multiplier=1).then_inc(acc_ok, 1)
            pool.affine_select(out=upto[:, :, :], in_=ones[0:1, 0:E * E].rearrange("o (f e) -> o f e", e=E),
                               compare_op=ALU.is_ge, fill=0.0, base=0,
                               pattern=[[1, E], [-1, E]], channel_multiplier=0).then_inc(const, 1)
            pool.iota(tile_no[:, :, :], [[1, TILES], [0, E]], base=0, channel_multiplier=0,
                      allow_small_or_imprecise_dtypes=True).then_inc(const, 1)
            pool.iota(tile_row[:, :], [[P, TILES]], base=0, channel_multiplier=0,
                      allow_small_or_imprecise_dtypes=True).then_inc(const, 1)
            pool.memset(fill[:, :], 0.0).then_inc(fill_ok, 1)
            pool.wait_ge(fill_ok, 1)
            pool.memset(fill_rows[:, :, 0:1], float(NO_TOKEN)).then_inc(fill_ok, 1)

            def batch(i):
                if i.plus(-1).within(B):
                    stats2(i.plus(-1))
                if i.plus(2).within(B):
                    stats1(i.plus(2))
                if i.plus(-2).within(B):
                    if i.plus(-2).at == 0 and i.turn is None:
                        pool.wait_ge(fill_st, 16)
                    file(i.plus(-2))
                if i.within(B):
                    name(i)

            run(pool, -2, B + 2, batch)
            pool.wait_ge(zero_st, 16)
            for s in range(2):
                pool.wait_ge(mid_st[s], 16 * (B // 2))

            def gather(t):
                b = t.slot(4)
                now = gathering.number(t)
                if t.at_least(4):
                    pool.wait_ge(y_ok, now - 4)
                pool.wait_ge(take_ok, now)
                gathering.begin(t)
                pool.indirect_dma_start(rows[:, b, :], None, mid,
                                        bass.IndirectOffsetOnAxis(take[:, b:b + 1], 0)).then_inc(row_ld[b], 16)

            def scatter(t):
                b = t.slot(4)
                now = scattering.number(t)
                pool.wait_ge(put_ok, now)
                pool.wait_ge(y_ok, now)
                scattering.begin(t)
                pool.indirect_dma_start(out, bass.IndirectOffsetOnAxis(put[:, b:b + 1], 0), res[:, b, :], None,
                                        bounds_check=N - 1, oob_is_err=False).then_inc(out_st[b], 16)

            def tile(i):
                if i.plus(3).within(TILES):
                    gather(i.plus(3))
                if i.within(TILES):
                    scatter(i)

            run(pool, -3, TILES, tile)

        @block.scalar
        def _(act):
            act.wait_ge(gate_ld, 32)
            act.activation(gate_th[:, :], gate_in[:, :], ACT.Tanh).then_inc(th_ok, 1)

            def ctx_part(j, k):
                act.wait_ge(ctxT_mm, j.times(4, k + 1))
                if k == 0 and j.at_least(2):
                    act.wait_ge(score_mm, j.times(1, -1))
                act.activation(ctxT[:, j.slot(2), k, :], ctx_ps[k % 2][:, 0:M], ACT.Copy).then_inc(ctxT_act, 1)

            def batch(i):
                j = i.plus(-2)
                if j.within(B):
                    act.wait_ge(lsh_ok, j.times(1, 1))
                    act.activation(lexp[:, :], lsh[:, j.slot(2), :], ACT.Exp,
                                   accum_out=lsum[:, j.slot(2):j.slot(2) + 1]).then_inc(lsum_ok, 1)
                j = i.plus(2)
                if j.within(B):
                    ctx_part(j, 0)
                j = i.plus(-1)
                if j.within(B):
                    act.wait_ge(xn2T_mm, j.times(1, 1))
                    if j.at_least(1):
                        act.wait_ge(lgT_mm, j.times(1))
                    act.activation(xn2T[:, :, :].rearrange("p k s -> p (k s)"), xT_ps[:, 0:KC * S], ACT.Copy
                                   ).then_inc(xn2T_ok, 1)
                j = i.plus(2)
                if j.within(B):
                    ctx_part(j, 2)
                    ctx_part(j, 3)
                j = i.plus(1)
                if j.within(B):
                    a = j.slot(2)
                    act.wait_ge(nbias_ok, j.times(1, 1))
                    if j.at_least(2):
                        act.wait_ge(prT_mm, j.times(1, -1))
                        act.wait_ge(rinv_ok, j.times(1, -1))
                    act.activation(pr[:, a, :], score_ps[a][0:S, 0:M], ACT.Exp, bias=nbias[:, a:a + 1], scale=SCALE,
                                   accum_out=psum_row[:, a:a + 1]).then_inc(pr_ok, 1)
                j = i.plus(-1)
                if j.within(B):
                    act.wait_ge(lgT_mm, j.times(1, 1))
                    if j.at_least(1):
                        act.wait_ge(lg_mm, j.times(1))
                    act.activation(lgT[:, :], lgT_ps, ACT.Copy).then_inc(lgT_ok, 1)
                j = i.plus(2)
                if j.within(B):
                    act.wait_ge(xnT_mm, j.times(1, 1))
                    act.activation(xnT[:, j.slot(2), :, :].rearrange("p k s -> p (k s)"), xT_ps[:, 0:KC * S],
                                   ACT.Copy).then_inc(xnT_ok, 1)

            run(act, -2, B + 2, batch)

        @block.vector
        def _(dve):
            dve.wait_ge(mask_ld, 16)
            dve.tensor_scalar(mask_add[:, :], mask_u8[:, :], -1.0, -MASKED, ALU.add, ALU.mult).then_inc(mask_ok, 1)
            dve.tensor_reduce(any_valid[:, :], mask_u8[:, :], AX.X, ALU.max).then_inc(mask_ok, 1)

            aggregating1 = Stage(dve, "aggregating1", 2)
            aggregating2 = Stage(dve, "aggregating2", -1)

            def stats1(j):
                a = j.slot(2)
                dve.wait_ge(x_ld[j.slot(4)], j.rounds(4) * 16 + 16)
                dve.bn_stats(st1[:, a, :], x_sb[:, j.slot(4), :]).then_inc(st1_ok, 1)

            def aggregate1(j):
                a = j.slot(2)
                now = aggregating1.number(j)
                if j.at_least(2):
                    dve.wait_ge(nm1_ok, j.times(1, -1))
                dve.wait_ge(st1_ok, now)
                aggregating1.begin(j)
                dve.bn_aggr(mv1[:, a, :], st1[:, a, :]).then_inc(mv1_ok, 1)

            def apply1(j):
                a = j.slot(2)
                dve.wait_ge(nm1_ok, j.times(1, 1))
                if j.at_least(2):
                    dve.wait_ge(xnT_mm, j.times(1, -1))
                dve.tensor_scalar(xn[:, a, :], x_sb[:, j.slot(4), :], ln1[:, a, 0:1], ln1[:, a, 1:2],
                                  ALU.mult, ALU.add).then_inc(xn_ok, 1)

            def apply2(j):
                a, b = j.slot(2), j.slot(4)
                dve.wait_ge(nm2_ok, j.times(1, 1))
                if j.at_least(2):
                    dve.wait_ge(xn2T_mm, j.times(1, -1))
                dve.tensor_scalar(xn2[:, a, :], x2[:, a, :], pay[:, b, 2:3], pay[:, b, 3:4],
                                  ALU.mult, ALU.add).then_inc(xn2_ok, 1)

            def set_up():
                dve.wait_ge(mask_ok, 2)
                dve.wait_ge(const, 11)
                dve.tensor_scalar(any_diag[:, :], ident[0:B, 0:B], any_valid[:, :], None, ALU.mult).then_inc(any_ok, 1)
                dve.wait_ge(b_ld, 16)
                dve.tensor_copy(b_part[0][:, :], b_raw[:, :]).then_inc(b_ok, 1)
                dve.wait_ge(b_ok, 1)
                dve.tensor_tensor(b_rest[0][:, :], b_raw[:, :], b_part[0][:, :], ALU.subtract).then_inc(b_ok, 1)
                dve.wait_ge(b_ok, 2)
                dve.tensor_copy(b_part[1][:, :], b_rest[0][:, :]).then_inc(b_ok, 1)
                dve.wait_ge(b_ok, 3)
                dve.tensor_tensor(b_rest[1][:, :], b_rest[0][:, :], b_part[1][:, :], ALU.subtract).then_inc(b_ok, 1)
                dve.wait_ge(b_ok, 4)
                dve.tensor_copy(b_part[2][:, :], b_rest[1][:, :]).then_inc(b_ok, 1)
                dve.wait_ge(valid_mm, 1)
                dve.wait_ge(th_ok, 1)
                dve.tensor_scalar(gv[:, :], valid_ps, gate_th[:, 0:1], None, ALU.mult).then_inc(gv_ok, 1)
                dve.wait_ge(gv_ok, 1)
                dve.wait_ge(acc_ok, 1)

            def residual(j):
                a = j.slot(2)
                if j.at_least(2):
                    dve.wait_ge(mid_st[a], j.rounds(2) * 16)
                dve.wait_ge(rscale_ok, j.times(1, 1))
                dve.wait_ge(read_mm, j.times(1, 1))
                dve.scalar_tensor_tensor(x2[:, a, :], read_ps[0:S, :], rscale[:, a:a + 1], x_sb[:, j.slot(4), :],
                                         ALU.mult, ALU.add).then_inc(x2_ok, 1)

            def stats2(j):
                dve.wait_ge(x2_ok, j.times(1, 1))
                dve.bn_stats(st2[:, j.slot(2), :], x2[:, j.slot(2), :]).then_inc(st2_ok, 1)

            def aggregate2(j):
                now = aggregating2.number(j)
                if j.at_least(2):
                    dve.wait_ge(nm2_ok, j.times(1, -1))
                dve.wait_ge(st2_ok, now)
                aggregating2.begin(j)
                dve.bn_aggr(mv2[:, j.slot(2), :], st2[:, j.slot(2), :]).then_inc(mv2_ok, 1)

            def choose(j, part):
                a = j.slot(2)
                if part == 0:
                    dve.wait_ge(lg_mm, j.times(1, 1))
                    dve.tensor_reduce(lmax[:, :], lg_ps, AX.X, ALU.max).then_inc(lmax_ok, 1)
                elif part == 1:
                    dve.wait_ge(lmax_ok, j.times(1, 1))
                    if j.at_least(2):
                        dve.wait_ge(lsum_ok, j.times(1, -1))
                    dve.tensor_scalar(lsh[:, a, :], lg_ps, lmax[:, :], None, ALU.subtract).then_inc(lsh_ok, 1)
                elif part == 2:
                    dve.wait_ge(lsh_ok, j.times(1, 1))
                    dve.scalar_tensor_tensor(key[:, :], lsh[:, a, :], 0.0, rev[0:S, :], ALU.is_ge, ALU.mult
                                             ).then_inc(key_ok, 1)
                elif part == 3:
                    dve.wait_ge(key_ok, j.times(1, 1))
                    dve.tensor_reduce(kmax[:, :], key[:, :], AX.X, ALU.max).then_inc(kmax_ok, 1)
                else:
                    dve.wait_ge(kmax_ok, j.times(1, 1))
                    dve.tensor_scalar(hot[:, a, :], key[:, :], kmax[:, :], None, ALU.is_equal).then_inc(hot_ok, 1)

            def place(j):
                a, b = j.slot(2), j.slot(4)
                dve.wait_ge(rank_mm, j.times(1, 1))
                dve.tensor_tensor(posm[:, :], rank_ps, hot[:, a, :], ALU.mult).then_inc(posm_ok, 1)
                dve.tensor_tensor(acc[0:S, :], acc[0:S, :], hot[:, a, :], ALU.add).then_inc(acc_ok, 1)
                dve.wait_ge(lsum_ok, j.times(1, 1))
                dve.reciprocal(linv[:, :], lsum[:, a:a + 1]).then_inc(linv_ok, 1)
                dve.wait_ge(posm_ok, j.times(1, 1))
                dve.tensor_reduce(pos_f[:, :], posm[:, :], AX.X, ALU.add).then_inc(posf_ok, 1)
                dve.wait_ge(id_ok, j.times(1, 1))
                dve.wait_ge(linv_ok, j.times(1, 1))
                dve.tensor_scalar(pay[:, b, 1:2], linv[:, :], gate_th[0:S, 1:2], None, ALU.mult
                                  ).then_inc(scale_ok, 1)
                dve.wait_ge(posf_ok, j.times(1, 1))
                dve.tensor_copy(pos[:, b:b + 1], pos_f[:, :]).then_inc(pos_ok, 1)

            def batch(i):
                read, gated, soon = i.plus(-1), i.plus(-2), i.plus(2)
                if read.within(B):
                    residual(read)
                if gated.within(B):
                    choose(gated, 0)
                if read.within(B):
                    stats2(read)
                if gated.within(B):
                    choose(gated, 1)
                if read.within(B):
                    aggregate2(read)
                if gated.within(B):
                    choose(gated, 2)
                    choose(gated, 3)
                if soon.within(B):
                    stats1(soon)
                if gated.within(B):
                    choose(gated, 4)
                if soon.within(B):
                    aggregate1(soon)
                j = i
                if j.within(B):
                    dve.wait_ge(prT_mm, j.times(1, 1))
                    if j.at_least(2):
                        dve.wait_ge(read_mm, j.times(1, -1))
                    dve.tensor_copy(prT[:, j.slot(2), :, :].rearrange("p c s -> p (c s)"), prob_ps[0:MP, 0:MC * S]
                                    ).then_inc(prT_ok, 1)
                if read.within(B):
                    apply2(read)
                j = i.plus(2)
                if j.within(B):
                    dve.wait_ge(ctxT_mm, j.times(4, 2))
                    if j.at_least(2):
                        dve.wait_ge(score_mm, j.times(1, -1))
                    dve.tensor_copy(ctxT[:, j.slot(2), 1, :], ctx_ps[1][:, 0:M]).then_inc(ctxT_dve, 1)
                if gated.within(B):
                    place(gated)
                if soon.within(B):
                    apply1(soon)
                j = i.plus(1)
                if j.within(B):
                    a = j.slot(2)
                    dve.wait_ge(score_mm, j.times(1, 1))
                    dve.tensor_reduce(nmax[:, a:a + 1], score_ps[a][0:S, 0:M], AX.X, ALU.max, negate=True
                                      ).then_inc(max_ok, 1)
                    dve.wait_ge(max_ok, j.times(1, 1))
                    if j.at_least(2):
                        dve.wait_ge(pr_ok, j.times(1, -1))
                    dve.tensor_scalar(nbias[:, a:a + 1], nmax[:, a:a + 1], SCALE, None, ALU.mult).then_inc(nbias_ok, 1)
                if i.turn is None and i.at == -1:
                    set_up()
                j = i
                if j.within(B):
                    a = j.slot(2)
                    dve.wait_ge(pr_ok, j.times(1, 1))
                    dve.reciprocal(rinv[:, a:a + 1], psum_row[:, a:a + 1]).then_inc(rinv_ok, 1)
                    dve.wait_ge(rinv_ok, j.times(1, 1))
                    dve.tensor_tensor(rscale[:, a:a + 1], rinv[:, a:a + 1], gv[0:S, bass.ds(j.times(1), 1)], ALU.mult
                                      ).then_inc(rscale_ok, 1)

            run(dve, -2, B + 2, batch)

            steps = [0]

            def step(ins):
                steps[0] += 1
                ins.then_inc(map_step, 1)
                dve.wait_ge(map_step, steps[0])

            dve.wait_ge(count_mm, 1)
            step(dve.tensor_scalar(cnt_i[:, :], count_ps, float(P - 1), None, ALU.add))
            step(dve.tensor_scalar(til_i[:, :], cnt_i[:, :], 7, None, ALU.arith_shift_right))
            step(dve.tensor_copy(til[:, :], til_i[:, :]))
            step(dve.tensor_tensor(cum3[:, :, :], upto[:, :, :], til[:, :].rearrange("o (f e) -> o f e", f=1).to_broadcast([1, E, E]), ALU.mult))
            step(dve.tensor_reduce(cum[:, :], cum3[:, :, :], AX.X, ALU.add))
            cum_all = cum[:, :].rearrange("o (f e) -> o f e", f=1).to_broadcast([1, TILES, E])
            step(dve.tensor_tensor(past[:, :, :], tile_no[:, :, :], cum_all, ALU.is_ge))
            step(dve.tensor_tensor(past_cum[:, :, :], past[:, :, :], cum_all, ALU.mult))
            step(dve.tensor_reduce(t_exp[:, :], past[:, :, :], AX.X, ALU.add))
            step(dve.tensor_reduce(t_start[:, :], past_cum[:, :, :], AX.X, ALU.max))
            step(dve.scalar_tensor_tensor(t_tmp[:, :], t_start[:, :], -float(P), tile_row[:, :], ALU.mult, ALU.add))
            step(dve.scalar_tensor_tensor(t_base[:, :], t_exp[:, :], float(REGION), t_tmp[:, :], ALU.mult, ALU.add))
            dve.tensor_scalar(tile_base[:, :], t_base[:, :], float(E * REGION), None, ALU.min).then_inc(map_ok, 1)
            dve.tensor_scalar(tile_expert[:, :], t_exp[:, :], float(E - 1), None, ALU.min).then_inc(map_ok, 1)

            def take_rows(t):
                dve.wait_ge(list_ld[t.slot(4)], t.rounds(4) * 16 + 16)
                if t.at_least(4):
                    dve.wait_ge(row_ld[t.slot(4)], t.rounds(4) * 16)
                dve.tensor_copy(take[:, t.slot(4):t.slot(4) + 1],
                                li[:, bass.ds(t.times(1), 1), 0:1].rearrange("p o c -> p (o c)")).then_inc(take_ok, 1)

            def tile(i):
                t = i.plus(4)
                if t.within(TILES):
                    take_rows(t)
                t = i.plus(1)
                if t.within(TILES):
                    dve.wait_ge(rnT_mm, t.times(1, 1))
                    if t.at_least(2):
                        dve.wait_ge(y_mm, t.times(1, -1))
                    dve.tensor_copy(rnT[:, t.slot(2), :], row_ps[t.slot(2)][:, :]).then_inc(rnT_ok, 1)
                t = i.plus(2)
                if t.within(TILES):
                    dve.wait_ge(row_ld[t.slot(4)], t.rounds(4) * 16 + 16)
                    if t.at_least(2):
                        dve.wait_ge(rnT_mm, t.times(1, -1))
                    dve.tensor_scalar(rn[:, t.slot(2), :], rows[:, t.slot(4), :],
                                      li[:, bass.ds(t.times(1), 1), 2:3].rearrange("p o c -> p (o c)"),
                                      li[:, bass.ds(t.times(1), 1), 3:4].rearrange("p o c -> p (o c)"),
                                      ALU.mult, ALU.add).then_inc(rn_ok, 1)
                t = i
                if t.within(TILES):
                    b = t.slot(4)
                    if t.at_least(4):
                        dve.wait_ge(out_st[b], t.rounds(4) * 16)
                    dve.tensor_copy(put[:, b:b + 1], li[:, bass.ds(t.times(1), 1), 0:1].rearrange("p o c -> p (o c)")
                                    ).then_inc(put_ok, 1)
                    dve.wait_ge(y_mm, t.times(1, 1))
                    dve.scalar_tensor_tensor(res[:, b, :], y_ps[t.slot(2)][:, :],
                                             li[:, bass.ds(t.times(1), 1), 1:2].rearrange("p o c -> p (o c)"),
                                             rows[:, b, :], ALU.mult, ALU.add).then_inc(y_ok, 1)

            run(dve, -4, TILES, tile)

        @block.tensor
        def _(pe):
            turning_logits = Stage(pe, "turning_logits", -1)

            def ctx_turn(j, k):
                if k == 0:
                    pe.wait_ge(ctx_ld[j.slot(4)], j.rounds(4) * 16 + 16)
                if k == 0 and j.at_least(1):
                    pe.wait_ge(ctxT_act, j.times(3, -1))
                if k == 1 and j.at_least(1):
                    pe.wait_ge(ctxT_act, j.times(3))
                if k == 2:
                    pe.wait_ge(ctxT_act, j.times(3, 1))
                if k == 3:
                    pe.wait_ge(ctxT_dve, j.times(1, 1))
                for c in range(MC):
                    last = pe.transpose(ctx_ps[k % 2][:, c * MP:(c + 1) * MP],
                                        ctx_sb[:, j.slot(4), c, k * P:(k + 1) * P], ident[0:MP, 0:MP])
                last.then_inc(ctxT_mm, 1)

            def x_turn(j):
                pe.wait_ge(xn_ok, j.times(1, 1))
                if j.turn is not None or j.at - 2 >= 1:
                    pe.wait_ge(xn2T_ok, j.times(1, -2))
                for k in range(KC):
                    last = pe.transpose(xT_ps[:, k * S:(k + 1) * S], xn[:, j.slot(2), k * P:(k + 1) * P],
                                        ident[0:S, 0:S])
                last.then_inc(xnT_mm, 1)

            def x2_turn(j):
                pe.wait_ge(xn2_ok, j.times(1, 1))
                pe.wait_ge(xnT_ok, j.times(1, 3) if j.turn is not None else min(j.at + 3, B))
                for k in range(KC):
                    last = pe.transpose(xT_ps[:, k * S:(k + 1) * S], xn2[:, j.slot(2), k * P:(k + 1) * P],
                                        ident[0:S, 0:S])
                last.then_inc(xn2T_mm, 1)

            def scores(j):
                a = j.slot(2)
                pe.wait_ge(xnT_ok, j.times(1, 1))
                pe.wait_ge(ctxT_act, j.times(3, 3))
                pe.wait_ge(ctxT_dve, j.times(1, 1))
                if j.at_least(2):
                    pe.wait_ge(pr_ok, j.times(1, -1))
                for k in range(KC):
                    pe.matmul(score_ps[a][0:S, 0:M], xnT[:, a, k, :], ctxT[:, a, k, :], start=(k == 0), stop=False)
                pe.matmul(score_ps[a][0:S, 0:M], ones_bf[0:1, 0:S], mask_row[0:1, bass.ds(j.times(M), M)],
                          start=False, stop=True).then_inc(score_mm, 1)

            def ranks(j):
                a = j.slot(2)
                pe.wait_ge(hot_ok, j.times(1, 1))
                pe.wait_ge(acc_ok, j.times(1, 1))
                pe.matmul(rank_ps, ones_bf[:, 0:S], acc[:, :], start=True, stop=False)
                pe.matmul(rank_ps, before[0:S, 0:S], hot[:, a, :], start=False, stop=True).then_inc(rank_mm, 1)

            def read_out(j, c):
                a = j.slot(2)
                if c == 0:
                    pe.wait_ge(prT_ok, j.times(1, 1))
                    if j.at_least(1):
                        pe.wait_ge(x2_ok, j.times(1))
                last = pe.matmul(read_ps[0:S, :], prT[:, a, c, :], ctx_sb[:, j.slot(4), c, :],
                                 start=(c == 0), stop=(c == MC - 1))
                if c == MC - 1:
                    last.then_inc(read_mm, 1)

            def batch(i):
                scored, now, turned, gated = i.plus(1), i, i.plus(2), i.plus(-1)
                if scored.within(B):
                    scores(scored)
                if i.plus(-2).within(B):
                    ranks(i.plus(-2))
                if now.within(B):
                    pe.wait_ge(pr_ok, now.times(1, 1))
                    if now.at_least(1):
                        pe.wait_ge(prT_ok, now.times(1))
                    for c in range(MC):
                        last = pe.transpose(prob_ps[0:MP, c * S:(c + 1) * S], pr[:, now.slot(2), c * MP:(c + 1) * MP],
                                            ident[0:S, 0:S])
                    last.then_inc(prT_mm, 1)
                if turned.within(B):
                    ctx_turn(turned, 0)
                    ctx_turn(turned, 1)
                if now.within(B):
                    read_out(now, 0)
                if gated.within(B):
                    x2_turn(gated)
                if turned.within(B):
                    ctx_turn(turned, 2)
                    ctx_turn(turned, 3)
                if now.within(B):
                    read_out(now, 1)
                if gated.within(B):
                    pe.wait_ge(xn2T_ok, gated.times(1, 1))
                    if gated.at_least(1):
                        pe.wait_ge(posm_ok, gated.times(1))
                    for k in range(KC):
                        last = pe.matmul(lgT_ps, wg_sb[:, k, :], xn2T[:, k, :], start=(k == 0), stop=(k == KC - 1))
                    last.then_inc(lgT_mm, 1)
                if turned.within(B):
                    x_turn(turned)
                if now.within(B):
                    read_out(now, 2)
                if gated.within(B):
                    pe.wait_ge(lgT_ok, turning_logits.number(gated))
                    turning_logits.begin(gated)
                    pe.transpose(lg_ps, lgT[:, :], ident[0:E, 0:E]).then_inc(lg_mm, 1)

            pe.wait_ge(const, 7)
            for n in range(-2, 0):
                batch(Count(n))
                if n == -2:
                    pe.wait_ge(mask_mv, 16)
            pe.wait_ge(any_ok, 1)
            pe.matmul(valid_ps, ones[0:B, :], any_diag[:, :], start=True, stop=True).then_inc(valid_mm, 1)
            pe.wait_ge(const, CONSTS - 3)
            pe.wait_ge(wg_ld, 16)
            pe.wait_ge(gv_ok, 1)
            run(pe, 0, B + 2, batch)

            pe.wait_ge(acc_ok, B + 1)
            pe.wait_ge(posm_ok, B)
            pe.matmul(count_ps, ones_bf[0:S, 0:1], acc[0:S, :], start=True, stop=True).then_inc(count_mm, 1)
            pe.wait_ge(w_ld, 16 * B)
            pe.wait_ge(b_mv, 48)
            pe.wait_ge(map_ok, 2)

            def tile(i):
                t = i.plus(1)
                if t.within(TILES):
                    a = t.slot(2)
                    pe.wait_ge(rn_ok, t.times(1, 1))
                    if t.at_least(2):
                        pe.wait_ge(rnT_ok, t.times(1, -1))
                    for k in range(KC):
                        last = pe.transpose(row_ps[a][:, k * P:(k + 1) * P], rn[:, a, k * P:(k + 1) * P], ident[:, :])
                    last.then_inc(rnT_mm, 1)
                t = i
                if t.within(TILES):
                    a = t.slot(2)
                    expert = pe.value_load(tile_expert[0:1, bass.ds(t.times(1), 1)], min_val=0, max_val=E - 1)
                    pe.wait_ge(rnT_ok, t.times(1, 1))
                    if t.at_least(2):
                        pe.wait_ge(y_ok, t.times(1, -1))
                    for k in range(KC):
                        pe.matmul(y_ps[a][:, :], rnT[:, a, k * P:(k + 1) * P],
                                  w_sb[:, bass.ds(expert * (KC * D) + k * D, D)], start=(k == 0), stop=False)
                    pe.matmul(y_ps[a][:, :], ones_bf[0:3, :], b3[:, bass.ds(expert * D, D)],
                              start=False, stop=True).then_inc(y_mm, 1)

            run(pe, -1, TILES, tile)


_INS = ["x", "ctx_2048", "mask_BxS2_bk0", "g_xattn", "g_ffn", "L0_ffn_Wg", "L0_ffn_W", "L0_ffn_b"]


def kernel(**inputs):
    import numpy as _np
    import concourse.bacc as _bacc
    from concourse import mybir as _mybir
    from concourse.bass_utils import run_bass_kernel_spmd as _run

    nc = _bacc.Bacc("TRN2", target_bir_lowering=False, num_devices=1)
    arrays, args = {}, []
    for name in _INS:
        a = _np.ascontiguousarray(inputs[name])
        if name == "L0_ffn_W":
            a = a.reshape(-1, a.shape[-1])
        arrays[f"in_{name}"] = a
        args.append(nc.dram_tensor(f"in_{name}", a.shape, _mybir.dt.from_np(a.dtype), kind="ExternalInput").ap())
    b, s, d = inputs["x"].shape
    out = nc.dram_tensor("out_rows", (b * s, d), _mybir.dt.float32, kind="ExternalOutput").ap()
    build(nc, *args, out)
    r = _run(nc, [arrays], core_ids=[0])
    return r.results[0]["out_rows"].reshape(b, s, d)
```

```python
from contextlib import ExitStack

import concourse.bass as bass
from concourse import mybir

F32 = mybir.dt.float32
F32R = mybir.dt.float32r
BF16 = mybir.dt.bfloat16
I32 = mybir.dt.int32
U32 = mybir.dt.uint32
U8 = mybir.dt.uint8
ALU = mybir.AluOpType
ACT = mybir.ActivationFunctionType
AX = mybir.AxisListType

P = 128
EPS = 1e-5
MASKED = -float(2**104)
TURN = 4


class Stage:

    def __init__(self, eng, name, shift):
        self.eng, self.reg = eng, eng.alloc_register(name)
        eng.reg_mov(self.reg, TURN + shift + 1)

    def number(self, j):
        return j.at + 1 if j.turn is None else self.eng.snap(self.reg)

    def begin(self, j):
        if j.turn is not None:
            self.eng.reg_add(self.reg, self.reg, 1)


class Count:

    def __init__(self, at, turn=None):
        self.at, self.turn = at, turn

    def plus(self, n):
        return Count(self.at + n, self.turn)

    def times(self, factor, more=0):
        if self.turn is None:
            return factor * self.at + more
        return self.turn * (factor * TURN) + (factor * self.at + more)

    def rounds(self, slots):
        if self.turn is None:
            return self.at // slots
        return self.turn * (TURN // slots) + self.at // slots

    def slot(self, slots):
        return self.at % slots

    def at_least(self, n):
        least = self.at if self.turn is None else TURN + self.at
        assert self.turn is None or least >= n
        return least >= n

    def within(self, n):
        return self.turn is not None or 0 <= self.at < n


def loop_end(last):
    return (last - 4) // TURN * TURN


def run(eng, first, last, body, loop_from=TURN):
    loop_to = loop_end(last)
    for n in range(first, loop_from):
        body(Count(n))
    with eng.Fori(loop_from // TURN, loop_to // TURN) as turn:
        for at in range(TURN):
            body(Count(at, turn))
    for n in range(loop_to, last):
        body(Count(n))


def build(nc, x, ctx, mask, g_attn, g_ffn, w_gate, w_exp, b_exp, out):
    B, S, D = x.shape
    M = ctx.shape[1]
    E = w_gate.shape[1]
    N = B * S
    KC = D // P
    MC = 3
    MP = M // MC
    ME = M + M % 2
    SCALE = 1.0 / float(D) ** 0.5
    REGION = 4096
    TILES = (N + E * (P - 1)) // P
    TAIL = loop_end(B + 2)
    SNAP = TAIL - 2
    EARLY = -(-(SNAP * S - E * (P - 1)) // P) // TURN * TURN
    NO_TOKEN = N
    LIST = E * REGION + P
    FILL = 64
    assert M == MC * MP and MP <= P and KC * S + E <= 512 and REGION >= N + P and B % TURN == 0 and S < P
    assert TAIL + TURN == B and 2 * TURN < EARLY < TILES

    x_rows = x.rearrange("b s d -> (b s) d")
    mid = nc.dram_tensor("mid_rows", (N + 1, D), F32, kind="Internal").ap()
    mask_rows = nc.dram_tensor("mask_rows", (B, M), BF16, kind="Internal").ap()
    lst = nc.dram_tensor("token_list", (LIST, 4), F32, kind="Internal").ap()

    with ExitStack() as stack:
        def sb(name, shape, dt=F32):
            return stack.enter_context(nc.sbuf_tensor(name, shape, dt))

        def ps(name):
            return stack.enter_context(nc.psum_tensor(name, [P, 512], F32))

        def sem(name):
            return stack.enter_context(nc.semaphore(name))

        ident = sb("ident", [P, P])
        ones = sb("ones", [P, P])
        ones_bf = sb("ones_bf", [P, P], BF16)
        before = sb("before", [P, P], BF16)
        half = sb("half", [P, 1])
        eps = sb("eps", [P, 1])
        minus = sb("minus", [P, 1])
        token_ids = sb("token_ids", [P, B], I32)
        b_pick = sb("b_pick", [3 * E, E, P], BF16)
        rev = sb("rev", [P, E])
        upto = sb("upto", [1, E, E])
        tile_no = sb("tile_no", [1, TILES - EARLY, E])
        tile_row = sb("tile_row", [1, TILES - EARLY])
        unused = sb("unused", [P, FILL, 4])
        zeros = sb("zeros", [1, P])
        w_raw = sb("w_raw", [P, 2, D])
        w_hi = sb("w_hi", [P, E * KC * D], F32R)
        w_lo = sb("w_lo", [P, E * KC * D], F32R)
        wg_sb = sb("wg_sb", [P, KC, E])
        b_part = [sb(f"b_part{i}", [E * KC, P], BF16) for i in range(3)]
        b_rows = sb("b_rows", [3 * E, D], BF16)
        mask_u8 = sb("mask_u8", [B, M], U8)
        mask_add = sb("mask_add", [B, M], BF16)
        mask_row = sb("mask_row", [1, 4, M], BF16)
        any_valid = sb("any_valid", [B, 1])
        any_diag = sb("any_diag", [B, B])
        gate_in = sb("gate_in", [P, 2])
        gate_th = sb("gate_th", [P, 2])
        gv = sb("gv", [P, B])
        x_sb = sb("x_sb", [S, 4, D])
        ctx_sb = sb("ctx_sb", [P, 4, MC, D])
        xn = sb("xn", [S, D])
        xnT_hi = sb("xnT_hi", [P, KC, S], F32R)
        xnT_lo = sb("xnT_lo", [P, KC, S], F32R)
        ctxT_hi = sb("ctxT_hi", [P, KC, ME], F32R)
        ctxT_lo = sb("ctxT_lo", [P, KC, ME], F32R)
        pr = sb("pr", [S, M])
        prT = sb("prT", [MP, MC, S])
        x2 = sb("x2", [S, D])
        xn2 = sb("xn2", [S, D])
        b_raw, b_rest = xn2[0:E * KC, 0:P], [xn2[0:E * KC, (i + 1) * P:(i + 2) * P] for i in range(2)]
        xn2T = sb("xn2T", [P, KC, S])
        st1 = sb("st1", [S, 2, 6])
        mv1 = sb("mv1", [S, 2, 2])
        ve1 = sb("ve1", [S, 2, 2])
        ln1 = sb("ln1", [S, 2, 2])
        st2 = sb("st2", [S, 2, 6])
        mv2 = sb("mv2", [S, 2, 2])
        ve2 = sb("ve2", [S, 2, 1])
        nmax = sb("nmax", [S, 2])
        nbias = sb("nbias", [S, 2])
        psum_row = sb("psum_row", [S, 2])
        rinv = sb("rinv", [S, 2])
        rscale = sb("rscale", [S, 2])
        lmax = sb("lmax", [S, 1])
        lsh = sb("lsh", [S, 2, E])
        lexp = sb("lexp", [S, E])
        lsum = sb("lsum", [S, 2])
        linv = sb("linv", [S, 1])
        key = sb("key", [S, E])
        kmax = sb("kmax", [S, 1])
        hot = sb("hot", [S, 2, E], BF16)
        acc = sb("acc", [P, E], BF16)
        acc_f = sb("acc_f", [P, E])
        posm = sb("posm", [S, E])
        pos_f = sb("pos_f", [S, 1])
        pos = sb("pos", [S, 4], U32)
        pay = sb("pay", [S, 4, 4])
        cnt_i = sb("cnt_i", [1, E], I32)
        til_i = sb("til_i", [1, E], I32)
        til = sb("til", [1, E])
        cum3 = sb("cum3", [1, E, E])
        cum = sb("cum", [1, E])
        cum_cut = sb("cum_cut", [1, E + 1])
        done = sb("done", [1, E + 1])
        left = sb("left", [1, E])
        jump = sb("jump", [1, E])
        first_row = sb("first_row", [1, 1])
        past = sb("past", [1, TILES - EARLY, E])
        past_jump = sb("past_jump", [1, TILES - EARLY, E])
        t_exp = sb("t_exp", [1, TILES - EARLY])
        t_jump = sb("t_jump", [1, TILES - EARLY])
        t_base = sb("t_base", [1, TILES - EARLY])
        tile_base = sb("tile_base", [1, TILES], I32)
        tile_expert = sb("tile_expert", [1, TILES], I32)
        li = sb("li", [P, TILES, 4])
        take = sb("take", [P, 4], U32)
        put = sb("put", [P, 4], U32)
        rows, res = ctx_sb[:, 0:4, 0, :], ctx_sb[:, 0:4, 1, :]
        rn = w_raw
        rnT_hi, rnT_lo = (part[:, :, :].rearrange("p k m -> p (k m)")[:, 0:2 * D].rearrange("p (a d) -> p a d", a=2)
                          for part in (ctxT_hi, ctxT_lo))

        ctx_ps = [ps("ctx_ps0"), ps("ctx_ps1")]
        score_ps = [ps("score_ps0"), ps("score_ps1")]
        read_ps = ps("read_ps")
        prob_ps = ps("prob_ps")
        xT_ps = prob_ps
        x2T_ps = ps("x2T_ps")
        small_ps = ps("small_ps")
        lg_ps = small_ps[0:S, P:P + E]
        rank_ps = small_ps[0:S, P + E:P + 2 * E]
        valid_ps = small_ps[:, 256:256 + B]
        count_ps = prob_ps[0:1, KC * S:KC * S + E]
        row_ps = ctx_ps
        prT_last = ctx_sb[0:MP, 0, 2, 0:MC * S].rearrange("p (c s) -> p c s", c=MC)
        read_last_ps = score_ps[(B - 2) % 2]

        def weights_of(j):
            return prT_last if j.turn is None and j.at == B - 1 else prT

        def read_out_of(j):
            return read_last_ps if j.turn is None and j.at == B - 1 else read_ps

        y_ps = score_ps

        gate_ld, wg_ld, b_ld, mask_ld = sem("gate_ld"), sem("wg_ld"), sem("b_ld"), sem("mask_ld")
        w_ld = [sem(f"w_ld{i}") for i in range(2)]
        w_hi_ok, w_lo_ok = sem("w_hi_ok"), sem("w_lo_ok")
        x_ld = [sem(f"x_ld{i}") for i in range(4)]
        ctx_ld = [sem(f"ctx_ld{i}") for i in range(4)]
        mask_in = [sem(f"mask_in{i}") for i in range(4)]
        fill_st, zero_st, mask_mv, b_mv = sem("fill_st"), sem("zero_st"), sem("mask_mv"), sem("b_mv")
        mid_st = [sem(f"mid_st{i}") for i in range(2)]
        list_st = [sem(f"list_st{i}") for i in range(4)]
        list_ld = [sem(f"list_ld{i}") for i in range(4)]
        row_ld = [sem(f"row_ld{i}") for i in range(4)]
        out_st = [sem(f"out_st{i}") for i in range(4)]
        const = sem("const")
        pick_ok, pad_ok = sem("pick_ok"), sem("pad_ok")
        fill_ok, zero_ok, mask_ok, b_ok = sem("fill_ok"), sem("zero_ok"), sem("mask_ok"), sem("b_ok")
        any_ok, valid_mm, th_ok, gv_ok = (sem(n) for n in ("any_ok", "valid_mm", "th_ok", "gv_ok"))
        st1_ok, mv1_ok, ve1_ok, rs1_ok, nm1_ok, xn_ok = (
            sem(n) for n in ("st1_ok", "mv1_ok", "ve1_ok", "rs1_ok", "nm1_ok", "xn_ok"))
        xnT_mm, xnT_ok = sem("xnT_mm"), sem("xnT_ok")
        ctxT_mm = sem("ctxT_mm")
        ctxT_hi_ok, ctxT_ok = sem("ctxT_hi_ok"), sem("ctxT_ok")
        xnT_hi_ok = sem("xnT_hi_ok")
        score_mm, max_ok, nbias_ok, pr_ok = sem("score_mm"), sem("max_ok"), sem("nbias_ok"), sem("pr_ok")
        prT_mm, prT_ok, read_mm = sem("prT_mm"), sem("prT_ok"), sem("read_mm")
        rinv_ok, rscale_ok, x2_ok = sem("rinv_ok"), sem("rscale_ok"), sem("x2_ok")
        st2_ok, mv2_ok, ve2_ok, rs2_ok, xn2_ok, id_ok = (
            sem(n) for n in ("st2_ok", "mv2_ok", "ve2_ok", "rs2_ok", "xn2_ok", "id_ok"))
        xn2T_mm, xn2T_ok, lg_mm = sem("xn2T_mm"), sem("xn2T_ok"), sem("lg_mm")
        lmax_ok, lsh_ok, lsum_ok, key_ok, kmax_ok, hot_ok = (
            sem(n) for n in ("lmax_ok", "lsh_ok", "lsum_ok", "key_ok", "kmax_ok", "hot_ok"))
        linv_ok, scale_ok, rank_mm, acc_ok, posm_ok, posf_ok, pos_ok = (
            sem(n) for n in ("linv_ok", "scale_ok", "rank_mm", "acc_ok", "posm_ok", "posf_ok", "pos_ok"))
        count_mm, count_ok, early_map_step, late_map_step, early_map_ok, late_map_ok = (
            sem(n) for n in ("count_mm", "count_ok", "early_map_step", "late_map_step", "early_map_ok", "late_map_ok"))
        rnT_hi_ok = sem("rnT_hi_ok")
        take_ok, put_ok, rn_ok, rnT_mm, rnT_ok, y_mm, y_ok = (
            sem(n) for n in ("take_ok", "put_ok", "rn_ok", "rnT_mm", "rnT_ok", "y_mm", "y_ok"))

        CONSTS = 16
        block = stack.enter_context(nc.Block())

        def make_map(eng, step, ok, late, part):
            tiles = TILES - EARLY if late else EARLY
            first = EARLY if late else 0
            if part == 1:
                step(eng.tensor_copy(til[:, :], til_i[:, :]))
                step(eng.tensor_tensor(jump[:, :], done[:, 1:E + 1], til[:, :], ALU.subtract))
                step(eng.tensor_tensor(left[:, :], til[:, :], done[:, 0:E], ALU.subtract))
            elif part == 2:
                step(eng.tensor_scalar(jump[:, :], jump[:, :], float(P), float(REGION), ALU.mult, ALU.add))
                step(eng.tensor_tensor(cum3[:, :, :], upto[:, :, :],
                                       left[:, :].rearrange("o (f e) -> o f e", f=1).to_broadcast([1, E, E]), ALU.mult))
                step(eng.tensor_reduce(cum[:, :], cum3[:, :, :], AX.X, ALU.add))
            elif part == 3:
                step(eng.tensor_tensor(past[:, 0:tiles, :], tile_no[:, 0:tiles, :],
                                       cum[:, :].rearrange("o (f e) -> o f e", f=1).to_broadcast([1, tiles, E]), ALU.is_ge))
                step(eng.tensor_reduce(t_exp[:, 0:tiles], past[:, 0:tiles, :], AX.X, ALU.add))
            elif part == 4:
                step(eng.tensor_tensor(past_jump[:, 0:tiles, :], past[:, 0:tiles, :],
                                       jump[:, :].rearrange("o (f e) -> o f e", f=1).to_broadcast([1, tiles, E]), ALU.mult))
                step(eng.tensor_reduce(t_jump[:, 0:tiles], past_jump[:, 0:tiles, :], AX.X, ALU.add))
            else:
                if late:
                    step(eng.tensor_scalar(first_row[:, :], done[:, 0:1], float(P), None, ALU.mult))
                    step(eng.tensor_scalar(t_jump[:, 0:tiles], t_jump[:, 0:tiles], first_row[:, :], None, ALU.add))
                step(eng.tensor_tensor(t_base[:, 0:tiles], tile_row[:, 0:tiles], t_jump[:, 0:tiles], ALU.add))
                eng.tensor_scalar(tile_base[:, first:first + tiles], t_base[:, 0:tiles], float(E * REGION), None,
                                  ALU.min).then_inc(ok, 1)
                eng.tensor_scalar(tile_expert[:, first:first + tiles], t_exp[:, 0:tiles], float(E - 1), None,
                                  ALU.min).then_inc(ok, 1)
                if not late:
                    step(eng.tensor_scalar(cum_cut[:, 1:E + 1], cum[:, :], float(EARLY), None, ALU.min))
                    eng.tensor_tensor(done[:, 0:E], cum_cut[:, 1:E + 1], cum_cut[:, 0:E], ALU.subtract).then_inc(ok, 1)

        @block.sync
        def _(sp):
            def load(j):
                sp.dma_start(x_sb[:, j.slot(4), :], x_rows[bass.ds(j.times(S), S), :]).then_inc(x_ld[j.slot(4)], 16)
                sp.dma_start(ctx_sb[0:MP, j.slot(4), :, :],
                             ctx[bass.ds(j.times(1), 1), :, :].rearrange("o (c p) d -> p (o c) d", c=MC)
                             ).then_inc(ctx_ld[j.slot(4)], 16)

            def load_mask(j):
                sp.dma_start(mask_row[:, j.slot(4), :], mask_rows[bass.ds(j.times(1), 1), :]
                             ).then_inc(mask_in[j.slot(4)], 16)

            def load_w(w):
                sp.dma_start(w_raw[:, w.slot(2), :], w_exp[bass.ds(w.times(P), P), :]).then_inc(w_ld[w.slot(2)], 16)

            sp.dma_start(mask_u8[:, :], mask).then_inc(mask_ld, 16)
            load(Count(0))
            sp.dma_start(gate_in[:, 0:1], g_attn.rearrange("(a b) -> a b", a=1).to_broadcast([P, 1])).then_inc(gate_ld, 16)
            sp.dma_start(gate_in[:, 1:2], g_ffn.rearrange("(a b) -> a b", a=1).to_broadcast([P, 1])).then_inc(gate_ld, 16)
            load(Count(1))
            sp.wait_ge(mask_ok, 2)
            sp.dma_start(mask_rows, mask_add[:, :]).then_inc(mask_mv, 16)
            sp.wait_ge(mask_mv, 16)
            for j in range(4):
                load_mask(Count(j))
            sp.dma_start(wg_sb[:, :, :], w_gate.rearrange("(k p) e -> p k e", p=P)).then_inc(wg_ld, 16)
            sp.dma_start(b_raw, b_exp.rearrange("e (c f) -> (e c) f", f=P)).then_inc(b_ld, 16)
            load_w(Count(0))
            load(Count(2))
            load(Count(3))
            load_w(Count(1))
            sp.wait_ge(fill_ok, 2)
            sp.dma_start(lst[0:E * REGION, :].rearrange("(p n r) c -> p n (r c)", p=P, r=FILL),
                         unused[:, :, :].rearrange("p (n r) c -> p n (r c)", n=1).to_broadcast([P, E * REGION // (P * FILL), FILL * 4])
                         ).then_inc(fill_st, 16)
            sp.dma_start(lst[E * REGION:LIST, :], unused[:, 0, :]).then_inc(fill_st, 16)
            sp.wait_ge(zero_ok, 1)
            sp.dma_start(mid[N:N + 1, :].rearrange("o (k p) -> o k p", p=P),
                         zeros[:, :].rearrange("o (k p) -> o k p", k=1).to_broadcast([1, KC, P])).then_inc(zero_st, 16)
            for i in range(3):
                sp.wait_ge(b_ok, (1, 3, 5)[i])
                sp.dma_start(b_rows[i * E:(i + 1) * E, :].rearrange("e (k p) -> e k p", p=P), b_part[i][:, :]
                             ).then_inc(b_mv, 16)

            def batch(i):
                if i.plus(2).within(B):
                    sp.wait_ge(w_lo_ok, i.times(1, 1))
                    load_w(i.plus(2))
                sp.wait_ge(x2_ok, i.times(1, 1))
                sp.dma_start(mid[bass.ds(i.times(S), S), :], x2[:, :]).then_inc(mid_st[i.slot(2)], 16)
                if i.plus(4).within(B):
                    load(i.plus(4))
                    load_mask(i.plus(4))

            run(sp, 0, B - 2, batch)

            def load_list(t):
                base = sp.value_load(tile_base[0:1, bass.ds(t.times(1), 1)], min_val=0, max_val=LIST - P)
                if t.at_least(4):
                    sp.wait_ge(take_ok, t.times(1, -3))
                sp.dma_start(li[:, bass.ds(t.times(1), 1), :].rearrange("p o c -> p (o c)"), lst[bass.ds(base, P), :]
                             ).then_inc(list_ld[t.slot(4)], 16)

            for s in range(4):
                sp.wait_ge(list_st[s], 16 * ((SNAP - s + 3) // 4))
            sp.wait_ge(early_map_ok, 2)
            for t in range(4):
                load_list(Count(t))
            for i in range(B - 2, B):
                batch(Count(i))
            for t in range(4, EARLY):
                load_list(Count(t))
            for s in range(2):
                sp.wait_ge(mid_st[s], 16 * (B // 2))
            for s in range(4):
                sp.wait_ge(list_st[s], 16 * (B // 4))
            sp.wait_ge(late_map_ok, 2)
            run(sp, EARLY, TILES, load_list, loop_from=EARLY)
            for s in range(4):
                sp.wait_ge(out_st[s], 16 * ((TILES - s + 3) // 4))

        @block.gpsimd
        def _(pool):
            pool.memset(ident[:, :], 0.0).then_inc(const, 1)
            pool.memset(ones_bf[:, :], 1.0).then_inc(const, 1)
            pool.memset(ones[:, :], 1.0).then_inc(const, 1)
            if ME > M:
                pool.memset(ctxT_hi[:, :, M:ME].bitcast(F32), 0.0).then_inc(pad_ok, 1)
                pool.memset(ctxT_lo[:, :, M:ME].bitcast(F32), 0.0).then_inc(pad_ok, 1)
            pool.memset(half[:, :], -0.5).then_inc(const, 1)
            pool.memset(eps[:, :], EPS).then_inc(const, 1)
            pool.memset(minus[:, :], -1.0).then_inc(const, 1)
            pool.wait_ge(const, 6)
            pool.affine_select(out=ident[:, :], in_=ident[:, :], compare_op=ALU.not_equal, fill=1.0, base=0,
                               pattern=[[-1, P]], channel_multiplier=1).then_inc(const, 1)

            filing = Stage(pool, "filing", -2)
            gathering = Stage(pool, "gathering", 4)
            scattering = Stage(pool, "scattering", 0)

            def split(w):
                pool.tensor_tensor(w_lo[:, bass.ds(w.times(D), D)], w_raw[:, w.slot(2), :],
                                   w_hi[:, bass.ds(w.times(D), D)].bitcast(F32), ALU.subtract).then_inc(w_lo_ok, 1)

            def stats1(j):
                a = j.slot(2)
                if j.at_least(2):
                    pool.wait_ge(xn_ok, j.times(1, -1))
                pool.wait_ge(mv1_ok, j.times(1, 1))
                pool.tensor_tensor(ve1[:, a, 0:1], mv1[:, a, 1:2], eps[0:S, :], ALU.add).then_inc(ve1_ok, 1)
                pool.tensor_tensor(ve1[:, a, 1:2], mv1[:, a, 0:1], minus[0:S, :], ALU.mult).then_inc(ve1_ok, 1)
                pool.wait_ge(ve1_ok, j.times(2, 1))
                pool.tensor_tensor(ln1[:, a, 0:1], ve1[:, a, 0:1], half[0:S, :], ALU.pow).then_inc(rs1_ok, 1)
                pool.wait_ge(ve1_ok, j.times(2, 2))
                pool.wait_ge(rs1_ok, j.times(1, 1))
                pool.tensor_tensor(ln1[:, a, 1:2], ve1[:, a, 1:2], ln1[:, a, 0:1], ALU.mult).then_inc(nm1_ok, 1)

            def name(j):
                b = j.slot(4)
                if j.at_least(4):
                    pool.wait_ge(list_st[b], j.rounds(4) * 16)
                pool.tensor_copy(pay[:, b, 0:1], token_ids[0:S, bass.ds(j.times(1), 1)]).then_inc(id_ok, 1)

            def stats2(j):
                a, b = j.slot(2), j.slot(4)
                w = j.plus(1)
                pool.wait_ge(mv2_ok, j.times(1, 1))
                pool.tensor_tensor(ve2[:, a, :], mv2[:, a, 1:2], eps[0:S, :], ALU.add).then_inc(ve2_ok, 1)
                pool.tensor_copy(pay[:, b, 3:4], mv2[:, a, 0:1])
                if w.within(B):
                    pool.wait_ge(w_ld[w.slot(2)], w.rounds(2) * 16 + 16)
                    pool.wait_ge(w_hi_ok, w.times(1, 1))
                pool.wait_ge(ve2_ok, j.times(1, 1))
                pool.tensor_tensor(pay[:, b, 2:3], ve2[:, a, :], half[0:S, :], ALU.pow).then_inc(rs2_ok, 1)
                if w.within(B):
                    split(w)

            def file(j):
                now = filing.number(j)
                pool.wait_ge(pos_ok, now)
                pool.wait_ge(scale_ok, now)
                filing.begin(j)
                pool.indirect_dma_start(lst, bass.IndirectOffsetOnAxis(pos[:, j.slot(4):j.slot(4) + 1], 0),
                                        pay[:, j.slot(4), :], None).then_inc(list_st[j.slot(4)], 16)

            pool.iota(token_ids[:, :], [[S, B]], base=0, channel_multiplier=1).then_inc(const, 1)
            pool.memset(zeros[:, :], 0.0).then_inc(zero_ok, 1)
            pool.affine_select(out=before[:, :], in_=ones_bf[:, :], compare_op=ALU.is_gt, fill=0.0, base=0,
                               pattern=[[1, P]], channel_multiplier=-1).then_inc(const, 1)
            pool.iota(rev[:, :], [[-1, E]], base=E, channel_multiplier=0,
                      allow_small_or_imprecise_dtypes=True).then_inc(const, 1)
            pool.iota(acc_f[:, :], [[REGION, E]], base=0, channel_multiplier=0,
                      allow_small_or_imprecise_dtypes=True).then_inc(const, 1)
            pool.wait_ge(const, 11)
            pool.affine_select(out=acc[:, :], in_=acc_f[:, :], compare_op=ALU.is_ge, fill=0.0, base=-(P - 1),
                               pattern=[[0, E]], channel_multiplier=1).then_inc(acc_ok, 1)
            pool.affine_select(out=upto[:, :, :], in_=ones[0:1, 0:E * E].rearrange("o (f e) -> o f e", e=E),
                               compare_op=ALU.is_ge, fill=0.0, base=0,
                               pattern=[[1, E], [-1, E]], channel_multiplier=0).then_inc(const, 1)
            pool.iota(tile_no[:, :, :], [[1, TILES - EARLY], [0, E]], base=0, channel_multiplier=0,
                      allow_small_or_imprecise_dtypes=True).then_inc(const, 1)
            pool.iota(tile_row[:, :], [[P, TILES - EARLY]], base=0, channel_multiplier=0,
                      allow_small_or_imprecise_dtypes=True).then_inc(const, 1)
            pool.memset(done[:, :], 0.0).then_inc(const, 1)
            pool.memset(cum_cut[:, 0:1], 0.0).then_inc(const, 1)
            def late_constants():
                pool.memset(b_pick[:, :, :], 0.0).then_inc(pick_ok, 1)
                for i in range(3):
                    pool.wait_ge(pick_ok, i + 1)
                    pool.affine_select(out=b_pick[:, :, :], in_=b_pick[:, :, :], compare_op=ALU.not_equal, fill=1.0,
                                       base=-E * i, pattern=[[-1, E], [0, P]], channel_multiplier=1).then_inc(pick_ok, 1)
                pool.memset(unused[:, :, :], 0.0).then_inc(fill_ok, 1)
                pool.wait_ge(fill_ok, 1)
                pool.memset(unused[:, :, 0:1], float(NO_TOKEN)).then_inc(fill_ok, 1)

            def batch(i):
                at = i.at if i.turn is None else 0
                if i.plus(-1).within(B):
                    stats2(i.plus(-1))
                elif i.within(B):
                    pool.wait_ge(w_ld[i.slot(2)], 16)
                    pool.wait_ge(w_hi_ok, 1)
                    split(i)
                if at in (B - 1, B + 1):
                    tile(Count(-2 if at == B - 1 else 1))
                if i.plus(-2).within(B):
                    if i.plus(-2).at == 0 and i.turn is None:
                        pool.wait_ge(fill_st, 32)
                    file(i.plus(-2))
                if i.within(B):
                    name(i)
                if i.plus(3).within(B):
                    stats1(i.plus(3))
                if at == -3:
                    late_constants()

            def gather(t):
                b = t.slot(4)
                now = gathering.number(t)
                if t.at_least(4):
                    pool.wait_ge(y_ok, now - 4)
                elif t.at == 0:
                    for s in range(2):
                        pool.wait_ge(mid_st[s], 16 * (SNAP // 2))
                if not t.at_least(4):
                    pool.wait_ge(read_mm, B - 3 + t.at)
                pool.wait_ge(take_ok, now)
                gathering.begin(t)
                source = mid[0:SNAP * S, :] if t.turn is None and t.at < 2 * TURN else mid
                pool.indirect_dma_start(rows[:, b, :], None, source,
                                        bass.IndirectOffsetOnAxis(take[:, b:b + 1], 0)).then_inc(row_ld[b], 16)

            def scatter(t):
                b = t.slot(4)
                now = scattering.number(t)
                pool.wait_ge(put_ok, now)
                pool.wait_ge(y_ok, now)
                scattering.begin(t)
                pool.indirect_dma_start(out, bass.IndirectOffsetOnAxis(put[:, b:b + 1], 0), res[:, b, :], None,
                                        bounds_check=N - 1, oob_is_err=False).then_inc(out_st[b], 16)

            def tile(i):
                if i.plus(4).within(TILES):
                    gather(i.plus(4))
                if i.within(TILES):
                    scatter(i)

            def batch_and_tiles(i):
                batch(i)
                at = i.at if i.turn is None else 0
                if at == B - 2:
                    tile(Count(-4))
                    tile(Count(-3))
                if at == B:
                    tile(Count(-1))
                    tile(Count(0))

            run(pool, -3, B + 2, batch_and_tiles)
            pool.wait_ge(zero_st, 16)
            for s in range(2):
                pool.wait_ge(mid_st[s], 16 * (B // 2))
            run(pool, 2, TILES, tile)

        @block.scalar
        def _(act):
            act.wait_ge(gate_ld, 32)
            act.activation(gate_th[:, :], gate_in[:, :], ACT.Tanh).then_inc(th_ok, 1)

            def ctx_part(j, k):
                act.wait_ge(ctxT_mm, j.times(4, k + 1))
                if k == 0 and j.at_least(1):
                    act.wait_ge(score_mm, j.times(1))
                act.activation(ctxT_hi[:, k, 0:M], ctx_ps[k % 2][:, 0:M], ACT.Copy).then_inc(ctxT_hi_ok, 1)

            def tile(t):
                act.wait_ge(rnT_mm, t.times(1, 1))
                if t.at_least(2):
                    act.wait_ge(y_mm, t.times(1, -1))
                act.activation(rnT_hi[:, t.slot(2), :], row_ps[t.slot(2)][:, :], ACT.Copy).then_inc(rnT_hi_ok, 1)

            def weights(j):
                a = j.slot(2)
                act.wait_ge(nbias_ok, j.times(1, 1))
                if j.at_least(1):
                    act.wait_ge(prT_mm, j.times(1))
                if j.at_least(2):
                    act.wait_ge(rinv_ok, j.times(1, -1))
                act.activation(pr[:, :], score_ps[a][0:S, 0:M], ACT.Exp, bias=nbias[:, a:a + 1], scale=SCALE,
                               accum_out=psum_row[:, a:a + 1]).then_inc(pr_ok, 1)

            def turned_weights(j):
                act.wait_ge(prT_mm, j.times(1, 1))
                if j.at_least(1) and weights_of(j) is prT:
                    act.wait_ge(read_mm, j.times(1))
                act.activation(weights_of(j)[:, :, :].rearrange("p c s -> p (c s)"), prob_ps[0:MP, 0:MC * S], ACT.Copy
                               ).then_inc(prT_ok, 1)

            def turned_x(j):
                act.wait_ge(xnT_mm, j.times(1, 1))
                if j.at_least(1):
                    act.wait_ge(score_mm, j.times(1))
                act.activation(xnT_hi[:, :, :].rearrange("p k s -> p (k s)"), xT_ps[:, 0:KC * S],
                               ACT.Copy).then_inc(xnT_hi_ok, 1)

            def apply1(j):
                a = j.slot(2)
                act.wait_ge(nm1_ok, j.times(1, 1))
                if j.at_least(1):
                    act.wait_ge(xnT_mm, j.times(1))
                act.activation(xn[:, :], x_sb[:, j.slot(4), :], ACT.Identity, bias=ln1[:, a, 1:2],
                               scale=ln1[:, a, 0:1]).then_inc(xn_ok, 1)

            def batch(i):
                at = i.at if i.turn is None else 0
                ahead, soon, gated = i.plus(1), i.plus(2), i.plus(-1)
                if at in (B, B + 1):
                    tile(Count(0 if at == B else 2))
                if at == B - 2:
                    turned_weights(i)
                if soon.within(B):
                    apply1(soon)
                j = i.plus(-2)
                if j.within(B):
                    act.wait_ge(lsh_ok, j.times(1, 1))
                    act.activation(lexp[:, :], lsh[:, j.slot(2), :], ACT.Exp,
                                   accum_out=lsum[:, j.slot(2):j.slot(2) + 1]).then_inc(lsum_ok, 1)
                if i.within(B) and at < B - 2:
                    turned_weights(i)
                if soon.within(B):
                    ctx_part(soon, 0)
                    ctx_part(soon, 1)
                if at == B - 2:
                    weights(ahead)
                if gated.within(B):
                    act.wait_ge(xn2T_mm, gated.times(1, 1))
                    if gated.at_least(1):
                        act.wait_ge(lg_mm, gated.times(1))
                    act.activation(xn2T[:, :, :].rearrange("p k s -> p (k s)"), x2T_ps[:, 0:KC * S], ACT.Copy
                                   ).then_inc(xn2T_ok, 1)
                if at == B:
                    tile(Count(1))
                if soon.within(B):
                    if at != -2:
                        turned_x(soon)
                    ctx_part(soon, 2)
                if ahead.within(B):
                    act.wait_ge(w_ld[ahead.slot(2)], ahead.rounds(2) * 16 + 16)
                if soon.within(B):
                    ctx_part(soon, 3)
                    if at == -2:
                        turned_x(soon)
                if ahead.within(B):
                    if at == B - 2:
                        turned_weights(ahead)
                    act.activation(w_hi[:, bass.ds(ahead.times(D), D)], w_raw[:, ahead.slot(2), :], ACT.Copy
                                   ).then_inc(w_hi_ok, 1)
                    if at != B - 2:
                        weights(ahead)

            run(act, -2, B + 2, batch)
            run(act, 3, TILES, tile)

        @block.vector
        def _(dve):
            dve.wait_ge(mask_ld, 16)
            dve.tensor_scalar(mask_add[:, :], mask_u8[:, :], -1.0, -MASKED, ALU.add, ALU.mult).then_inc(mask_ok, 1)
            dve.tensor_reduce(any_valid[:, :], mask_u8[:, :], AX.X, ALU.max).then_inc(mask_ok, 1)

            aggregating1 = Stage(dve, "aggregating1", 3)
            aggregating2 = Stage(dve, "aggregating2", -1)

            def stats1(j):
                a = j.slot(2)
                dve.wait_ge(x_ld[j.slot(4)], j.rounds(4) * 16 + 16)
                dve.bn_stats(st1[:, a, :], x_sb[:, j.slot(4), :]).then_inc(st1_ok, 1)

            def aggregate1(j):
                a = j.slot(2)
                now = aggregating1.number(j)
                if j.at_least(2):
                    dve.wait_ge(nm1_ok, j.times(1, -1))
                dve.wait_ge(st1_ok, now)
                aggregating1.begin(j)
                dve.bn_aggr(mv1[:, a, :], st1[:, a, :]).then_inc(mv1_ok, 1)

            def which_valid():
                dve.wait_ge(mask_ok, 2)
                dve.wait_ge(const, 7)
                dve.tensor_scalar(any_diag[:, :], ident[0:B, 0:B], any_valid[:, :], None, ALU.mult).then_inc(any_ok, 1)
                dve.wait_ge(valid_mm, 1)
                dve.wait_ge(th_ok, 1)
                dve.tensor_scalar(gv[:, :], valid_ps, gate_th[:, 0:1], None, ALU.mult).then_inc(gv_ok, 1)

            def split_biases():
                dve.wait_ge(b_ld, 16)
                dve.tensor_copy(b_part[0][:, :], b_raw).then_inc(b_ok, 1)
                dve.wait_ge(b_ok, 1)
                dve.tensor_tensor(b_rest[0], b_raw, b_part[0][:, :], ALU.subtract).then_inc(b_ok, 1)
                dve.wait_ge(b_ok, 2)
                dve.tensor_copy(b_part[1][:, :], b_rest[0]).then_inc(b_ok, 1)
                dve.wait_ge(b_ok, 3)
                dve.tensor_tensor(b_rest[1], b_rest[0], b_part[1][:, :], ALU.subtract).then_inc(b_ok, 1)
                dve.wait_ge(b_ok, 4)
                dve.tensor_copy(b_part[2][:, :], b_rest[1]).then_inc(b_ok, 1)
                dve.wait_ge(gv_ok, 1)
                dve.wait_ge(const, 11)
                dve.wait_ge(acc_ok, 1)

            def residual(j):
                a = j.slot(2)
                if j.at_least(1):
                    before = j.plus(-1)
                    dve.wait_ge(mid_st[before.slot(2)], before.rounds(2) * 16 + 16)
                dve.wait_ge(rscale_ok, j.times(1, 1))
                dve.wait_ge(read_mm, j.times(1, 1))
                dve.scalar_tensor_tensor(x2[:, :], read_out_of(j)[0:S, :], rscale[:, a:a + 1], x_sb[:, j.slot(4), :],
                                         ALU.mult, ALU.add).then_inc(x2_ok, 1)

            def stats2(j):
                dve.wait_ge(x2_ok, j.times(1, 1))
                dve.bn_stats(st2[:, j.slot(2), :], x2[:, :]).then_inc(st2_ok, 1)

            def aggregate2(j):
                now = aggregating2.number(j)
                if j.at_least(2):
                    dve.wait_ge(rs2_ok, j.times(1, -1))
                dve.wait_ge(st2_ok, now)
                aggregating2.begin(j)
                dve.bn_aggr(mv2[:, j.slot(2), :], st2[:, j.slot(2), :]).then_inc(mv2_ok, 1)

            def choose(j, part):
                a = j.slot(2)
                if part == 0:
                    dve.wait_ge(lg_mm, j.times(1, 1))
                    dve.tensor_reduce(lmax[:, :], lg_ps, AX.X, ALU.max).then_inc(lmax_ok, 1)
                elif part == 1:
                    dve.wait_ge(lmax_ok, j.times(1, 1))
                    if j.at_least(2):
                        dve.wait_ge(lsum_ok, j.times(1, -1))
                    dve.tensor_scalar(lsh[:, a, :], lg_ps, lmax[:, :], None, ALU.subtract).then_inc(lsh_ok, 1)
                elif part == 2:
                    dve.wait_ge(lsh_ok, j.times(1, 1))
                    dve.scalar_tensor_tensor(key[:, :], lsh[:, a, :], 0.0, rev[0:S, :], ALU.is_ge, ALU.mult
                                             ).then_inc(key_ok, 1)
                elif part == 3:
                    dve.wait_ge(key_ok, j.times(1, 1))
                    dve.tensor_reduce(kmax[:, :], key[:, :], AX.X, ALU.max).then_inc(kmax_ok, 1)
                else:
                    dve.wait_ge(kmax_ok, j.times(1, 1))
                    dve.tensor_scalar(hot[:, a, :], key[:, :], kmax[:, :], None, ALU.is_equal).then_inc(hot_ok, 1)

            def place(j):
                a, b = j.slot(2), j.slot(4)
                dve.wait_ge(rank_mm, j.times(1, 1))
                dve.tensor_tensor(posm[:, :], rank_ps, hot[:, a, :], ALU.mult).then_inc(posm_ok, 1)
                dve.tensor_tensor(acc[0:S, :], acc[0:S, :], hot[:, a, :], ALU.add).then_inc(acc_ok, 1)
                dve.wait_ge(lsum_ok, j.times(1, 1))
                dve.reciprocal(linv[:, :], lsum[:, a:a + 1]).then_inc(linv_ok, 1)
                dve.wait_ge(posm_ok, j.times(1, 1))
                dve.tensor_reduce(pos_f[:, :], posm[:, :], AX.X, ALU.add).then_inc(posf_ok, 1)
                dve.wait_ge(id_ok, j.times(1, 1))
                dve.wait_ge(linv_ok, j.times(1, 1))
                dve.tensor_scalar(pay[:, b, 1:2], linv[:, :], gate_th[0:S, 1:2], None, ALU.mult
                                  ).then_inc(scale_ok, 1)
                dve.wait_ge(posf_ok, j.times(1, 1))
                dve.tensor_copy(pos[:, b:b + 1], pos_f[:, :]).then_inc(pos_ok, 1)

            def take_rows(t):
                dve.wait_ge(list_ld[t.slot(4)], t.rounds(4) * 16 + 16)
                if t.at_least(4):
                    dve.wait_ge(row_ld[t.slot(4)], t.rounds(4) * 16)
                dve.tensor_copy(take[:, t.slot(4):t.slot(4) + 1],
                                li[:, bass.ds(t.times(1), 1), 0:1].rearrange("p o c -> p (o c)")).then_inc(take_ok, 1)

            def tile(i):
                t = i.plus(4)
                if t.within(TILES):
                    take_rows(t)
                t = i.plus(1)
                if t.within(TILES):
                    dve.wait_ge(rnT_mm, t.times(1, 1))
                    if t.at_least(2):
                        dve.wait_ge(y_mm, t.times(1, -1))
                    dve.wait_ge(rnT_hi_ok, t.times(1, 1))
                    dve.tensor_tensor(rnT_lo[:, t.slot(2), :], row_ps[t.slot(2)][:, :],
                                      rnT_hi[:, t.slot(2), :].bitcast(F32), ALU.subtract).then_inc(rnT_ok, 1)
                t = i.plus(2)
                if t.within(TILES):
                    dve.wait_ge(row_ld[t.slot(4)], t.rounds(4) * 16 + 16)
                    if t.at_least(2):
                        dve.wait_ge(rnT_mm, t.times(1, -1))
                    dve.tensor_scalar(rn[:, t.slot(2), :], rows[:, t.slot(4), :],
                                      li[:, bass.ds(t.times(1), 1), 3:4].rearrange("p o c -> p (o c)"),
                                      li[:, bass.ds(t.times(1), 1), 2:3].rearrange("p o c -> p (o c)"),
                                      ALU.subtract, ALU.mult).then_inc(rn_ok, 1)
                t = i
                if t.within(TILES):
                    b = t.slot(4)
                    if t.at_least(4):
                        dve.wait_ge(out_st[b], t.rounds(4) * 16)
                    dve.tensor_copy(put[:, b:b + 1], li[:, bass.ds(t.times(1), 1), 0:1].rearrange("p o c -> p (o c)")
                                    ).then_inc(put_ok, 1)
                    dve.wait_ge(y_mm, t.times(1, 1))
                    dve.scalar_tensor_tensor(res[:, b, :], y_ps[t.slot(2)][:, :],
                                             li[:, bass.ds(t.times(1), 1), 1:2].rearrange("p o c -> p (o c)"),
                                             rows[:, b, :], ALU.mult, ALU.add).then_inc(y_ok, 1)

            early_steps, late_steps = [0], [0]

            def early_step(ins):
                early_steps[0] += 1
                ins.then_inc(early_map_step, 1)
                dve.wait_ge(early_map_step, early_steps[0])

            def late_step(ins):
                late_steps[0] += 1
                ins.then_inc(late_map_step, 1)
                dve.wait_ge(late_map_step, late_steps[0])

            def read_counts(late):
                dve.wait_ge(count_mm, late + 1)
                dve.wait_ge(prT_ok, B if late else TAIL + 1)
                dve.tensor_scalar(cnt_i[:, :], count_ps, float(P - 1) if late else 0.0, None, ALU.add
                                  ).then_inc(count_ok, 1)
                dve.wait_ge(count_ok, 2 * late + 1)
                dve.tensor_scalar(til_i[:, :], cnt_i[:, :], 7, None, ALU.arith_shift_right).then_inc(count_ok, 1)

            def batch_and_tiles(i):
                at = i.at if i.turn is None else 0
                batch(i)
                if at == TAIL:
                    dve.wait_ge(count_ok, 2)
                    make_map(dve, early_step, early_map_ok, 0, 1)
                if at == TAIL + 1:
                    for part in range(2, 6):
                        make_map(dve, early_step, early_map_ok, 0, part)
                if at == B - 2:
                    tile(Count(-4))
                    tile(Count(-3))
                if at == B:
                    tile(Count(0))

            def apply2(j):
                dve.wait_ge(rs2_ok, j.times(1, 1))
                if j.at_least(1):
                    dve.wait_ge(xn2T_mm, j.times(1))
                dve.tensor_scalar(xn2[:, :], x2[:, :], mv2[:, j.slot(2), 0:1], pay[:, j.slot(4), 2:3],
                                  ALU.subtract, ALU.mult).then_inc(xn2_ok, 1)

            def low_part(j, k):
                dve.wait_ge(ctxT_hi_ok, j.times(4, k + 1))
                dve.tensor_tensor(ctxT_lo[:, k, 0:M], ctx_ps[k % 2][:, 0:M], ctxT_hi[:, k, 0:M].bitcast(F32), ALU.subtract
                                  ).then_inc(ctxT_ok, 1)

            def greatest(j):
                a = j.slot(2)
                dve.wait_ge(score_mm, j.times(1, 1))
                dve.tensor_reduce(nmax[:, a:a + 1], score_ps[a][0:S, 0:M], AX.X, ALU.max, negate=True
                                  ).then_inc(max_ok, 1)

            def exp_bias(j):
                a = j.slot(2)
                dve.wait_ge(max_ok, j.times(1, 1))
                if j.at_least(2):
                    dve.wait_ge(pr_ok, j.times(1, -1))
                dve.tensor_scalar(nbias[:, a:a + 1], nmax[:, a:a + 1], SCALE, None, ALU.mult).then_inc(nbias_ok, 1)

            def batch(i):
                at = i.at if i.turn is None else 0
                read, gated, soon, later = i.plus(-1), i.plus(-2), i.plus(2), i.plus(3)
                a = i.slot(2)
                if read.within(B):
                    residual(read)
                if at == B:
                    dve.wait_ge(w_lo_ok, B)
                    tile(Count(-1))
                if gated.within(B):
                    choose(gated, 0)
                if read.within(B):
                    stats2(read)
                if gated.within(B):
                    choose(gated, 1)
                if i.within(B):
                    dve.wait_ge(pr_ok, i.times(1, 1))
                    dve.reciprocal(rinv[:, a:a + 1], psum_row[:, a:a + 1]).then_inc(rinv_ok, 1)
                if read.within(B):
                    aggregate2(read)
                if gated.within(B):
                    choose(gated, 2)
                if i.within(B):
                    dve.wait_ge(rinv_ok, i.times(1, 1))
                    dve.tensor_tensor(rscale[:, a:a + 1], rinv[:, a:a + 1], gv[0:S, bass.ds(i.times(1), 1)], ALU.mult
                                      ).then_inc(rscale_ok, 1)
                if gated.within(B):
                    choose(gated, 3)
                    choose(gated, 4)
                if at == TAIL:
                    read_counts(0)
                if i.plus(1).within(B) and at != -1:
                    greatest(i.plus(1))
                if read.within(B):
                    apply2(read)
                if i.plus(1).within(B) and at != -1:
                    exp_bias(i.plus(1))
                if soon.within(B):
                    low_part(soon, 0)
                    low_part(soon, 1)
                if at == B + 1:
                    tile(Count(1))
                if at == B - 1:
                    dve.wait_ge(w_lo_ok, B - 1)
                    tile(Count(-2))
                if gated.within(B):
                    place(gated)
                if soon.within(B) and at != -2:
                    turned_x(soon)
                if soon.within(B):
                    low_part(soon, 2)
                if later.within(B) and at != -1:
                    stats1(later)
                if soon.within(B):
                    low_part(soon, 3)
                if at == -1:
                    greatest(Count(0))
                    stats1(later)
                    exp_bias(Count(0))
                if soon.within(B) and at == -2:
                    turned_x(soon)
                if later.within(B):
                    aggregate1(later)
                if at == -3:
                    which_valid()
                if at == -1:
                    split_biases()

            def turned_x(j):
                dve.wait_ge(xnT_hi_ok, j.times(1, 1))
                dve.tensor_tensor(xnT_lo[:, :, :].rearrange("p k s -> p (k s)"), xT_ps[:, 0:KC * S],
                                  xnT_hi[:, :, :].rearrange("p k s -> p (k s)").bitcast(F32), ALU.subtract
                                  ).then_inc(xnT_ok, 1)

            run(dve, -3, B + 2, batch_and_tiles)
            for n in range(2, 2 * TURN):
                tile(Count(n))
                if n == 2:
                    read_counts(1)
                    dve.wait_ge(count_ok, 4)
                    dve.wait_ge(early_map_ok, 3)
                if n < 7:
                    make_map(dve, late_step, late_map_ok, 1, n - 1)
            run(dve, 2 * TURN, TILES, tile, loop_from=2 * TURN)

        @block.tensor
        def _(pe):
            def ctx_turn(j, k, gated=None):
                if k == 0:
                    pe.wait_ge(ctx_ld[j.slot(4)], j.rounds(4) * 16 + 16)
                if k >= 2 or j.at_least(1):
                    pe.wait_ge(ctxT_ok, j.times(4, k - 1))
                for c in range(MC):
                    last = pe.transpose(ctx_ps[k % 2][:, c * MP:(c + 1) * MP],
                                        ctx_sb[0:MP, j.slot(4), c, k * P:(k + 1) * P], ident[0:MP, 0:MP])
                    if c == MC - 1:
                        last.then_inc(ctxT_mm, 1)
                    if gated is not None:
                        gate(gated, c)

            def x_turn(j):
                pe.wait_ge(xn_ok, j.times(1, 1))
                for k in range(KC):
                    last = pe.transpose(xT_ps[:, k * S:(k + 1) * S], xn[:, k * P:(k + 1) * P],
                                        ident[0:S, 0:S])
                last.then_inc(xnT_mm, 1)

            def x2_turn(j):
                pe.wait_ge(xn2_ok, j.times(1, 1))
                for k in range(KC):
                    last = pe.transpose(x2T_ps[:, k * S:(k + 1) * S], xn2[:, k * P:(k + 1) * P],
                                        ident[0:S, 0:S])
                last.then_inc(xn2T_mm, 1)

            def gate(j, k):
                if k == 0:
                    pe.wait_ge(xn2T_ok, j.times(1, 1))
                    if j.at_least(1):
                        pe.wait_ge(posm_ok, j.times(1))
                last = pe.matmul(lg_ps, xn2T[:, k, :], wg_sb[:, k, :], start=(k == 0), stop=(k == KC - 1))
                if k == KC - 1:
                    last.then_inc(lg_mm, 1)

            def scores(j):
                a = j.slot(2)
                pe.wait_ge(xnT_ok, j.times(1, 1))
                pe.wait_ge(ctxT_ok, j.times(4, 4))
                for k in range(KC):
                    pe.matmul(score_ps[a][0:S, 0:ME], xnT_hi[:, k, :], ctxT_hi[:, k, :], start=(k == 0), stop=False)
                    pe.matmul(score_ps[a][0:S, 0:ME], xnT_lo[:, k, :], ctxT_hi[:, k, :], start=False, stop=False)
                    pe.matmul(score_ps[a][0:S, 0:ME], xnT_hi[:, k, :], ctxT_lo[:, k, :], start=False, stop=False)
                pe.wait_ge(mask_in[j.slot(4)], j.rounds(4) * 16 + 16)
                pe.matmul(score_ps[a][0:S, 0:M], ones_bf[0:1, 0:S], mask_row[0:1, j.slot(4), :],
                          start=False, stop=True).then_inc(score_mm, 1)

            def turn_weights(j):
                pe.wait_ge(pr_ok, j.times(1, 1))
                for c in range(MC):
                    last = pe.transpose(prob_ps[0:MP, c * S:(c + 1) * S], pr[:, c * MP:(c + 1) * MP],
                                        ident[0:S, 0:S])
                last.then_inc(prT_mm, 1)

            def ranks(j):
                a = j.slot(2)
                pe.wait_ge(hot_ok, j.times(1, 1))
                pe.wait_ge(acc_ok, j.times(1, 1))
                pe.matmul(rank_ps, ones_bf[:, 0:S], acc[:, :], start=True, stop=False)
                pe.matmul(rank_ps, before[0:S, 0:S], hot[:, a, :], start=False, stop=True).then_inc(rank_mm, 1)

            def read_out(j, c):
                a = j.slot(2)
                if c == 0:
                    pe.wait_ge(prT_ok, j.times(1, 1))
                    if j.at_least(1) and read_out_of(j) is read_ps:
                        pe.wait_ge(x2_ok, j.times(1))
                last = pe.matmul(read_out_of(j)[0:S, :], weights_of(j)[:, c, :], ctx_sb[0:MP, j.slot(4), c, :],
                                 start=(c == 0), stop=(c == MC - 1))
                if c == MC - 1:
                    last.then_inc(read_mm, 1)

            def expert_of(t):
                return pe.value_load(tile_expert[0:1, bass.ds(t.times(1), 1)], min_val=0, max_val=E - 1)

            def tile(i):
                expert = expert_of(i) if i.within(TILES) else None
                turn_rows(i.plus(1))
                products(i, expert)

            def turn_rows(t):
                if t.within(TILES):
                    a = t.slot(2)
                    pe.wait_ge(rn_ok, t.times(1, 1))
                    if t.at_least(2):
                        pe.wait_ge(rnT_ok, t.times(1, -1))
                    for k in range(KC):
                        last = pe.transpose(row_ps[a][:, k * P:(k + 1) * P], rn[:, a, k * P:(k + 1) * P], ident[:, :])
                    last.then_inc(rnT_mm, 1)

            def products(t, expert, then=None):
                if t.within(TILES):
                    a = t.slot(2)
                    pe.wait_ge(rnT_ok, t.times(1, 1))
                    if t.at_least(2):
                        pe.wait_ge(y_ok, t.times(1, -1))
                    if t.turn is None and t.at < 2:
                        pe.wait_ge(x2_ok, B)
                    for k in range(KC):
                        chunk = bass.ds(expert * (KC * D) + k * D, D)
                        if then is not None and k == KC - 1:
                            then()
                        hi, lo = rnT_hi[:, a, k * P:(k + 1) * P], rnT_lo[:, a, k * P:(k + 1) * P]
                        pe.matmul(y_ps[a][:, :], hi, w_hi[:, chunk], start=(k == 0), stop=False)
                        pe.matmul(y_ps[a][:, :], lo, w_hi[:, chunk], start=False, stop=False)
                        pe.matmul(y_ps[a][:, :], hi, w_lo[:, chunk], start=False, stop=False)
                    pe.matmul(y_ps[a][:, :], b_pick[:, bass.ds(expert, 1), :].rearrange("q o p -> q (o p)"), b_rows[:, :],
                              start=False, stop=True).then_inc(y_mm, 1)

            def count():
                pe.matmul(count_ps, ones_bf[0:S, 0:1], acc[0:S, :], start=True, stop=True).then_inc(count_mm, 1)

            def last_turns():
                ranks(Count(B - 2))
                x2_turn(Count(B - 1))
                turn_rows(Count(1))

            def batch(i):
                if i.turn is None and i.at == B:
                    pe.wait_ge(w_lo_ok, B)
                    pe.wait_ge(pick_ok, 4)
                    pe.wait_ge(b_mv, 48)
                    pe.wait_ge(early_map_ok, 2)
                    products(Count(0), expert_of(Count(0)), last_turns)
                if i.turn is None and i.at == B + 1:
                    tile(Count(1))
                at = i.at if i.turn is None else 0
                scored, now, turned, gated = i.plus(1), i, i.plus(2), i.plus(-1)
                if at == -1:
                    ctx_turn(turned, 0)
                    ctx_turn(turned, 1)
                if at == B - 2:
                    pe.wait_ge(xnT_ok, B)
                    turn_weights(now)
                if scored.within(B):
                    scores(scored)
                if at == TAIL:
                    pe.wait_ge(acc_ok, SNAP + 1)
                    count()
                if at == TAIL + 1:
                    pe.wait_ge(count_ok, 1)
                if now.within(B) and at < B - 2:
                    turn_weights(now)
                if turned.within(B) and at != -1:
                    ctx_turn(turned, 0)
                    ctx_turn(turned, 1)
                if at == B - 1:
                    for c in range(MC):
                        read_out(now, c)
                if at == B - 2:
                    read_out(now, 0)
                    read_out(now, 1)
                if i.plus(-2).within(B) and at != B:
                    ranks(i.plus(-2))
                if now.within(B) and at < B - 2:
                    read_out(now, 0)
                if gated.within(B) and at != B:
                    x2_turn(gated)
                if at == B - 1:
                    tile(Count(-1))
                if turned.within(B):
                    if at != -2:
                        x_turn(turned)
                    ctx_turn(turned, 2)
                    ctx_turn(turned, 3, gated if gated.within(B) else None)
                    if at == -2:
                        x_turn(turned)
                if at == B - 2:
                    read_out(now, 2)
                    turn_weights(scored)
                if gated.within(B):
                    for k in range(MC if turned.within(B) else 0, KC):
                        gate(gated, k)
                if now.within(B) and at < B - 2:
                    read_out(now, 1)
                if now.within(B) and at < B - 2:
                    read_out(now, 2)

            pe.wait_ge(const, 7)
            if ME > M:
                pe.wait_ge(pad_ok, 2)
            pe.wait_ge(any_ok, 1)
            pe.matmul(valid_ps, ones[0:B, :], any_diag[:, :], start=True, stop=True).then_inc(valid_mm, 1)
            for n in range(-2, 0):
                batch(Count(n))
            pe.wait_ge(const, CONSTS - 3)
            pe.wait_ge(wg_ld, 16)
            pe.wait_ge(gv_ok, 1)
            run(pe, 0, B + 2, batch)

            tile(Count(2))
            pe.wait_ge(acc_ok, B + 1)
            count()
            for t in range(3, 2 * TURN):
                tile(Count(t))
            pe.wait_ge(late_map_ok, 2)
            run(pe, 2 * TURN, TILES, tile, loop_from=2 * TURN)


_INS = ["x", "ctx_2048", "mask_BxS2_bk0", "g_xattn", "g_ffn", "L0_ffn_Wg", "L0_ffn_W", "L0_ffn_b"]


def kernel(**inputs):
    import numpy as _np
    import concourse.bacc as _bacc
    from concourse import mybir as _mybir
    from concourse.bass_utils import run_bass_kernel_spmd as _run

    nc = _bacc.Bacc("TRN2", target_bir_lowering=False, num_devices=1)
    arrays, args = {}, []
    for name in _INS:
        a = _np.ascontiguousarray(inputs[name])
        if name == "L0_ffn_W":
            a = a.reshape(-1, a.shape[-1])
        arrays[f"in_{name}"] = a
        args.append(nc.dram_tensor(f"in_{name}", a.shape, _mybir.dt.from_np(a.dtype), kind="ExternalInput").ap())
    b, s, d = inputs["x"].shape
    out = nc.dram_tensor("out_rows", (b * s, d), _mybir.dt.float32, kind="ExternalOutput").ap()
    build(nc, *args, out)
    r = _run(nc, [arrays], core_ids=[0])
    return r.results[0]["out_rows"].reshape(b, s, d)
```
